# Optimizing a Trainium2 kernel written in Bass

```python
import numpy as np
import jax
import jax.numpy as jnp

def _softmax(x, axis=-1):
    return jax.nn.softmax(x, axis=axis)

def _gelu(x):
    return jax.nn.gelu(x, approximate=True)

def _silu(x):
    return jax.nn.silu(x)

def _sigmoid(x):
    return jax.nn.sigmoid(x)

def _layernorm(x, axis=-1, eps=1e-05):
    m = jnp.mean(x, axis=axis, keepdims=True)
    v = jnp.var(x, axis=axis, keepdims=True)
    return (x - m) / jnp.sqrt(v + eps)

def _scatter_add(tgt, idx, src, axis=0):
    return tgt.at[idx].add(src)

def _segment_sum(src, seg, n):
    return jax.ops.segment_sum(src, seg, n)
kernel_name = 'mk_prb_d1_jaxref_r8_dc11f1'

def setup_inputs(seed: int=0):
    np.random.seed(seed)
    _w = jnp.asarray

    def _L0_attn_setup():
        import jax, jax.numpy as jnp
        import numpy as np
        D_MODEL = 128
        SCALE = float(np.sqrt(D_MODEL))
        key = jax.random.key(seed)
        k1, k2, k3 = jax.random.split(key, 3)
        input_data = jax.random.normal(k1, (4, 256, D_MODEL), dtype=jnp.float32)
        qk = jax.random.normal(k2, (D_MODEL, D_MODEL), dtype=jnp.float32) / SCALE
        ov = jax.random.normal(k3, (D_MODEL, D_MODEL), dtype=jnp.float32) / SCALE
        return {'input_data': input_data, 'qk': qk, 'ov': ov}
    _L0_attn_in = _L0_attn_setup()

    def _L0_ffn_setup():
        import jax, jax.numpy as jnp
        import numpy as np
        B, S, D, F, E = (8, 128, 128, 512, 8)
        EPS = 1e-05
        key = jax.random.key(seed)
        ks = jax.random.split(key, 4)
        s = 0.02
        return {'input_features': jax.random.normal(ks[0], (B, S, D), jnp.float32), 'centroids': jax.random.normal(ks[1], (E, D), jnp.float32) * 0.1, 'ln_g': jnp.ones((E, D), jnp.float32), 'ln_b': jnp.zeros((E, D), jnp.float32), 'w1': jax.random.normal(ks[2], (E, D, F), jnp.float32) * s, 'b1': jnp.zeros((E, F), jnp.float32), 'w2': jax.random.normal(ks[3], (E, F, D), jnp.float32) * s, 'b2': jnp.zeros((E, D), jnp.float32)}
    _L0_ffn_in = _L0_ffn_setup()
    _d = {'L0_attn_input_data': _L0_attn_in['input_data'], 'L0_attn_qk': _L0_attn_in['qk'], 'L0_attn_ov': _L0_attn_in['ov'], 'L0_ffn_centroids': _L0_ffn_in['centroids'], 'L0_ffn_ln_g': _L0_ffn_in['ln_g'], 'L0_ffn_ln_b': _L0_ffn_in['ln_b'], 'L0_ffn_w1': _L0_ffn_in['w1'], 'L0_ffn_b1': _L0_ffn_in['b1'], 'L0_ffn_w2': _L0_ffn_in['w2'], 'L0_ffn_b2': _L0_ffn_in['b2']}
    _x0 = _d['L0_attn_input_data']
    _d['L0_attn_input_data'] = jax.random.normal(jax.random.fold_in(jax.random.key(seed), 1), (2, 2048, 128), dtype=_x0.dtype)
    del _x0
    return _d

def reference(L0_attn_input_data, L0_attn_qk, L0_attn_ov, L0_ffn_centroids, L0_ffn_ln_g, L0_ffn_ln_b, L0_ffn_w1, L0_ffn_b1, L0_ffn_w2, L0_ffn_b2):

    def _L0_attn_ref(input_data, qk, ov):
        import jax, jax.numpy as jnp
        import numpy as np
        D_MODEL = 128
        SCALE = float(np.sqrt(D_MODEL))
        S = input_data.shape[1]
        scores = jnp.einsum('bsd,de,bte->bst', input_data, qk, input_data) / SCALE
        causal = jnp.tril(jnp.ones((S, S), dtype=bool))
        scores = jnp.where(causal, scores, -jnp.inf)
        attn = jax.nn.softmax(scores, axis=-1)
        return jnp.einsum('bst,btd,de->bse', attn, input_data, ov)

    def _L0_ffn_ref(input_features, centroids, ln_g, ln_b, w1, b1, w2, b2):
        import jax, jax.numpy as jnp
        import numpy as np
        B, S, D, F, E = (8, 128, 128, 512, 8)
        EPS = 1e-05
        x = input_features.reshape(-1, D)
        aff = jax.lax.stop_gradient(x @ centroids.T)
        eid = jnp.argmax(aff, axis=-1)
        alpha = jax.nn.sigmoid(jnp.sum(x * centroids[eid], axis=-1, keepdims=True))
        mu = jnp.mean(x, axis=-1, keepdims=True)
        var = jnp.mean((x - mu) ** 2, axis=-1, keepdims=True)
        xn = (x - mu) * jax.lax.rsqrt(var + EPS)
        xln = xn * ln_g[eid] + ln_b[eid]
        onehot = jax.nn.one_hot(eid, E, dtype=x.dtype)
        ffn = jnp.zeros_like(x)
        for e in range(E):
            h = jax.nn.relu(xln @ w1[e] + b1[e])
            ffn = ffn + onehot[:, e:e + 1] * (h @ w2[e] + b2[e])
        out = x + alpha * ffn
        return out.reshape(input_features.shape)
    x = L0_attn_input_data
    xn = _layernorm(x, axis=-1)
    x = x + _L0_attn_ref(xn, L0_attn_qk, L0_attn_ov) + _L0_ffn_ref(xn, L0_ffn_centroids, L0_ffn_ln_g, L0_ffn_ln_b, L0_ffn_w1, L0_ffn_b1, L0_ffn_w2, L0_ffn_b2)
    return x

_drawn_inputs = setup_inputs


def setup_inputs(seed=0):
    import zlib

    import numpy as np

    out = dict(_drawn_inputs(seed))
    spreads = {'L0_ffn_ln_g': (1.0, 0.6),
     'L0_ffn_ln_b': (0.0, 2.0),
     'L0_ffn_b1': (0.0, 0.635),
     'L0_ffn_b2': (0.0, 0.1)}
    factors = {}
    for name, (base, spread) in spreads.items():
        noise = np.random.default_rng([zlib.crc32(name.encode()), seed]).standard_normal(out[name].shape)
        drawn = base * np.exp(spread * noise) if base else spread * noise
        out[name] = jnp.asarray(drawn.astype(out[name].dtype))
    for name, factor in factors.items():
        out[name] = (out[name] * factor).astype(out[name].dtype)
    return out
```

```python
import concourse.bass as bass
from concourse import mybir
from contextlib import ExitStack

F32 = mybir.dt.float32
F16 = mybir.dt.float16
BF16 = mybir.dt.bfloat16
I32 = mybir.dt.int32
U32 = mybir.dt.uint32
ALU = mybir.AluOpType
ACT = mybir.ActivationFunctionType
AX = mybir.AxisListType

P = 128
EPS = 1e-5
W_SCALE = 16.0
QK_SCALE = 64.0
SHIFT = 32.0
MASK = -1e30
LAST = P - 1


def flat(ap):
    return ap.rearrange("p a b -> p (a b)")


def build(nc, x, qk, ov, cent, ln_g, ln_b, w1, b1, w2, b2, sorted_x, sorted_y, out):
    B, S, D = x.shape
    E, _, F = w1.shape
    assert D == P
    N = B * S
    NT = N // P
    GT = 4
    GW = GT * P
    NG = N // GW
    BG = S // GW
    BT = S // P
    FC = F // P
    FT = 2
    FW = FT * P
    NS = NT // FT + E
    UNITS = [GT * (g + 1) for g in range(BG)]
    STEPS = sum(UNITS)
    SCALE = float(D) ** -0.5

    x_t = x.rearrange("b (t p) d -> p (b t) d", p=P)
    out_t = out.rearrange("b (t p) d -> p (b t) d", p=P)

    with ExitStack() as ctx:
        def sb(name, shape, dt=F32):
            return ctx.enter_context(nc.sbuf_tensor(name, shape, dt))

        def sem(name):
            return ctx.enter_context(nc.semaphore(name))

        x_sb = sb("x_sb", [P, NT, P])
        xn = sb("xn", [P, NT, P])
        yg = xn
        xa_hi = sb("xa_hi", [P, NT, P], F16)
        xa_lo = sb("xa_lo", [P, NT, P], F16)
        x2 = sb("x2", [P, NT, 2 * P], F16)
        kT_hi = sb("kT_hi", [P, N], F16)
        kT_lo = sb("kT_lo", [P, N], F16)
        qT_hi = sb("qT_hi", [P, N], F16)
        qT_lo = sb("qT_lo", [P, N], F16)
        w_raw = sb("w_raw", [P, 2, F])
        w1_hl = sb("w1_hl", [P, E, 2 * F], F16)
        w2_hl = sb("w2_hl", [P, E, 2 * F], F16)
        b1_sb = sb("b1_sb", [1, E * F])
        b2_sb = sb("b2_sb", [2, E * P])
        b2_hi = sb("b2_hi", [2, E * P], F16)
        b2_lo = sb("b2_lo", [2, E * P])
        b2_hl = sb("b2_hl", [2, E * P], F16)
        small = sb("small", [3 * 8, P])
        smallT = sb("smallT", [P, 3 * 8])
        cent_hi = sb("cent_hi", [P, E], F16)
        cent_lo = sb("cent_lo", [P, E], F16)
        qk_sb = sb("qk_sb", [P, P])
        ov_sb = sb("ov_sb", [P, P])
        ovC = sb("ovC", [P, P + 1])
        U_sb = sb("U_sb", [P, P])
        G_hi = sb("G_hi", [P, P], F16)
        G_lo = sb("G_lo", [P, P], F16)
        A_e = sb("A_e", [P, 2, P])
        ident = sb("ident", [P, P])
        ident16 = sb("ident16", [P, P], F16)
        CT = sb("CT", [P, P])
        onesf = sb("onesf", [P, P])
        ones16 = sb("ones16", [P, P], F16)
        upper = sb("upper", [P, P], F16)
        mask_qk = sb("mask_qk", [P, P], BF16)
        mask_kq = sb("mask_kq", [P, P], BF16)
        stats = sb("stats", [P, 2, 6])
        mv = sb("mv", [P, NT, 2])
        vs = sb("vs", [P, 2, 2, NT])
        rs = sb("rs", [P, 2, NT])
        nw = sb("nw", [P, 2, 2, NT])
        aff = sb("aff", [P, NT, E])
        amax = sb("amax", [P, NT])
        eneg = sb("eneg", [P, NT])
        alpha = sb("alpha", [P, NT])
        hit = sb("hit", [P, NT, E])
        rank_w = sb("rank_w", [P, E])
        onehot = sb("onehot", [P, NT, E])
        onehot16 = sb("onehot16", [P, NT, E], F16)
        cum = sb("cum", [P, 2, NT, E])
        below = sb("below", [P, NT, E])
        cnt = sb("cnt", [P, E])
        cnt_i = sb("cnt_i", [P, E], I32)
        tiles_i = sb("tiles_i", [P, E], I32)
        tiles_f = sb("tiles_f", [P, E])
        tcum = sb("tcum", [P, 2, E])
        base = sb("base", [P, E])
        posf = sb("posf", [P, NT])
        pos = sb("pos", [P, NT], U32)
        slot = sb("slot", [1, NS, E])
        slot_hit = sb("slot_hit", [1, NS, E])
        tile_ef = sb("tile_ef", [1, NS])
        tile_e = sb("tile_e", [1, NS + 4], I32)
        zero = sb("zero", [P, 2 * P], F16)
        row_max = sb("row_max", [P, GT, BG])
        row_m = sb("row_m", [P, GT])
        neg_max = sb("neg_max", [P, GT, P], F16)
        p_sb = sb("p_sb", [P, 2, GW])
        p_hi = sb("p_hi", [P, 2, GW], F16)
        p_lo = sb("p_lo", [P, 2, GW], F16)
        oT = sb("oT", [P, GW])
        inv_den = sb("inv_den", [P, 2, 2])
        xs_sb = sb("xs_sb", [P, 2, FT, 2 * P], F16)
        x2T = sb("x2T", [P, 2, 2 * FW], F16)
        h_hi = sb("h_hi", [P, 2, FC * FW], F16)
        h_lo = sb("h_lo", [P, 2, FC * FW], F16)
        y_sb = sb("y_sb", [P, 2, FT * P])
        row16 = sb("row16", [2, P], F16)
        last_row = sb("last_row", [1, P])

        psum = ctx.enter_context(nc.psum_tensor("psum", [P, 8, 512], F32))
        bank = [psum[:, i, :] for i in range(8)]

        s_xin = [sem(f"s_xin{i}") for i in range(NG)]
        s_win = sem("s_win")
        s_wl = [sem("s_wl0"), sem("s_wl1")]
        s_const = sem("s_const")
        s_dve = sem("s_dve")
        s_actc = sem("s_actc")
        s_small = sem("s_small")
        s_smallc = sem("s_smallc")
        s_xa = sem("s_xa")
        s_basep = sem("s_basep")
        s_x2hi = sem("s_x2hi")
        s_xahi = sem("s_xahi")
        s_xalo = sem("s_xalo")
        s_kp = sem("s_kp")
        s_khi = sem("s_khi")
        s_klo = sem("s_klo")
        s_phi = sem("s_phi")
        s_plo = sem("s_plo")
        s_pvlo = sem("s_pvlo")
        s_qp = sem("s_qp")
        s_qhi = sem("s_qhi")
        s_qlo = sem("s_qlo")
        s_affp = sem("s_affp")
        s_Ae = sem("s_Ae")
        s_w1p = sem("s_w1p")
        s_w1hi = sem("s_w1hi")
        s_w1lo = sem("s_w1lo")
        s_w2hi = sem("s_w2hi")
        s_w2lo = sem("s_w2lo")
        s_cnt = sem("s_cnt")
        s_onehot = sem("s_onehot")
        s_pos = sem("s_pos")
        s_tile_e = sem("s_tile_e")
        s_zero = sem("s_zero")
        s_zeroed = sem("s_zeroed")
        s_scat = sem("s_scat")
        s_max_mm = sem("s_max_mm")
        s_max = sem("s_max")
        s_neg = sem("s_neg")
        s_negT = sem("s_negT")
        s_shift = sem("s_shift")
        s_sc = sem("s_sc")
        s_exp = sem("s_exp")
        s_pv = sem("s_pv")
        s_oT = sem("s_oT")
        s_fin = sem("s_fin")
        s_att = sem("s_att")
        s_xs = [sem(f"s_xs{i}") for i in range(2)]
        s_tr = sem("s_tr")
        s_x2T = sem("s_x2T")
        s_z = sem("s_z")
        s_hhi = sem("s_hhi")
        s_hlo = sem("s_hlo")
        s_y = sem("s_y")
        s_ysb = sem("s_ysb")
        s_yst = [sem(f"s_yst{i}") for i in range(2)]
        s_gath = sem("s_gath")
        s_sum = sem("s_sum")
        s_out = sem("s_out")
        s_dve_roots = sem("s_dve_roots")
        s_x2lo = sem("s_x2lo")
        s_aug = sem("s_aug")
        s_Aw = sem("s_Aw")
        s_amax = sem("s_amax")

        def tile(t, i, n=P):
            return flat(t[:, bass.ds(i, 1), :])

        xn_g, hi_g, lo_g = (t[:].rearrange("p (g t) d -> p g (t d)", t=GT) for t in (xn, xa_hi, xa_lo))

        w1_flat, w2_flat = (flat(t[:]) for t in (w1_hl, w2_hl))
        hidden_ps = [psum[:, 2 * u:2 * u + 2, :].rearrange("p a b -> p (a b)") for u in range(2)]

        def cols(t, i, n=GW):
            return t[:, bass.ds(i * n, n)]

        def wait(eng, s, n):
            if not isinstance(n, int) or n > 0:
                eng.wait_ge(s, n)

        block = ctx.enter_context(nc.Block())

        @block.sync
        def _(sp):
            for dst, src in ((small[0:8, :], cent), (small[8:16, :], ln_g), (small[16:24, :], ln_b),
                             (qk_sb[:], qk), (ov_sb[:], ov),
                             (b1_sb[:], b1.rearrange("(o e) f -> o (e f)", o=1)),
                             (b2_sb[0:1, :], b2.rearrange("(o e) f -> o (e f)", o=1)),
                             (b2_sb[1:2, :], b2.rearrange("(o e) f -> o (e f)", o=1))):
                sp.dma_start(dst, src).then_inc(s_win, 16)
            for g in range(NG):
                sp.dma_start(x_sb[:, g * GT:(g + 1) * GT, :], x_t[:, g * GT:(g + 1) * GT, :]).then_inc(s_xin[g], 16)
            sp.wait_ge(s_zero, 1)
            sp.dma_start(sorted_x.rearrange("(p a) d -> p a d", p=P),
                         zero[:, :].unsqueeze(1).broadcast_to([P, NS * FT, 2 * P])).then_inc(s_zeroed, 16)
            for e in range(E):
                if e:
                    sp.wait_ge(s_w1p, e)
                sp.dma_start(w_raw[:, 0, :], w1[e, :, :]).then_inc(s_wl[0], 16)
                if e:
                    sp.wait_ge(s_w2hi, e)
                    sp.wait_ge(s_w2lo, e)
                sp.dma_start(w_raw[:, 1, :].rearrange("p (c d) -> p c d", d=P),
                             w2[e, :, :].rearrange("(c p) d -> p c d", p=P)).then_inc(s_wl[1], 16)
            sp.wait_ge(s_scat, 16 * NT)
            src = sorted_x.rearrange("(k t p) d -> k p t d", p=P, t=FT)
            dst = sorted_y.rearrange("(k t p) d -> k p t d", p=P, t=FT)

            def block_of(t, k):
                return (t[bass.ds(k, 1), :, :, :]).rearrange("k p t d -> p (k t) d")

            def load_sorted(k, u):
                sp.dma_start(xs_sb[:, u, :, :], block_of(src, k)).then_inc(s_xs[u], 16)

            def store_sorted(k, u):
                sp.wait_ge(s_ysb, k + 1)
                sp.dma_start(block_of(dst, k), y_sb[:, u, :].rearrange("p (t d) -> p t d", d=P)).then_inc(s_yst[u], 16)

            def move(k, u):
                if not isinstance(k, int) or k < NS:
                    wait(sp, s_tr, k - 1)
                    load_sorted(k, u)
                if not isinstance(k, int) or k >= 4:
                    store_sorted(k - 4, u)

            for k in range(4):
                move(k, k % 2)
            with sp.Fori(2, NS // 2) as r:
                for u in range(2):
                    move(r * 2 + u, u)
            for k in range(NS, NS + 4):
                move(k, k % 2)
            for g in range(NG):
                sp.wait_ge(s_sum, g + 1)
                sp.dma_start(out_t[:, g * GT:(g + 1) * GT, :], x_sb[:, g * GT:(g + 1) * GT, :]).then_inc(s_out, 16)
            sp.wait_ge(s_out, 16 * NG)

        @block.gpsimd
        def _(pool):
            pool.memset(zero[:], 0.0).then_inc(s_zero, 1)
            pool.memset(onesf[:], 1.0).then_inc(s_const, 1)
            pool.memset(CT[:], 0.0).then_inc(s_const, 1)
            pool.memset(neg_max[:], 0.0).then_inc(s_const, 1)
            pool.memset(row16[:], W_SCALE).then_inc(s_const, 1)
            pool.memset(tile_e[:], 0).then_inc(s_const, 1)
            pool.iota(rank_w[:], pattern=[[-1, E]], base=E, channel_multiplier=0,
                      allow_small_or_imprecise_dtypes=True).then_inc(s_const, 1)
            pool.iota(slot[:], pattern=[[1, NS], [0, E]], base=0, channel_multiplier=0,
                      allow_small_or_imprecise_dtypes=True).then_inc(s_const, 1)
            n = 7
            pool.wait_ge(s_const, n)
            row = [[1, P]]
            pool.affine_select(out=ident[:], in_=onesf[:], compare_op=ALU.is_equal, fill=0.0, base=0,
                               pattern=row, channel_multiplier=-1).then_inc(s_const, 1)
            pool.affine_select(out=ident16[:], in_=onesf[:], compare_op=ALU.is_equal, fill=0.0, base=0,
                               pattern=row, channel_multiplier=-1).then_inc(s_const, 1)
            pool.affine_select(out=upper[:], in_=onesf[:], compare_op=ALU.is_gt, fill=0.0, base=0,
                               pattern=row, channel_multiplier=-1).then_inc(s_const, 1)
            pool.affine_select(out=ones16[:], in_=onesf[:], compare_op=ALU.is_ge, fill=0.0, base=0,
                               pattern=row, channel_multiplier=0).then_inc(s_const, 1)
            pool.affine_select(out=mask_qk[:], in_=CT[:], compare_op=ALU.is_ge, fill=MASK, base=0,
                               pattern=[[-1, P]], channel_multiplier=1).then_inc(s_const, 1)
            pool.affine_select(out=mask_kq[:], in_=CT[:], compare_op=ALU.is_ge, fill=MASK, base=0,
                               pattern=row, channel_multiplier=-1).then_inc(s_const, 1)
            pool.affine_select(out=last_row[:], in_=onesf[0:1, :], compare_op=ALU.is_ge, fill=0.0, base=-LAST,
                               pattern=row, channel_multiplier=0).then_inc(s_const, 1)
            n += 7
            pool.wait_ge(s_const, n)
            pool.affine_select(out=CT[:], in_=ident[:], compare_op=ALU.is_gt, fill=-1.0, base=LAST,
                               pattern=[[0, P]], channel_multiplier=-1).then_inc(s_const, 1)
            n += 1
            pool.wait_ge(s_const, n)
            pool.affine_select(out=CT[:], in_=CT[:], compare_op=ALU.is_gt, fill=0.0, base=LAST,
                               pattern=[[-1, P]], channel_multiplier=0).then_inc(s_const, 1)
            for h in range(2):
                pool.wait_ge(s_xa, NT // 2 * (h + 1))
                with pool.Fori(h * NG // 2, (h + 1) * NG // 2) as g:
                    both = x_sb[:, bass.ds(g * GT, GT), :]
                    pool.tensor_tensor(out=both, in0=both, in1=xn[:, bass.ds(g * GT, GT), :], op=ALU.add).then_inc(s_basep, 1)
            pool.wait_ge(s_zeroed, 16)
            pool.wait_ge(s_pos, 1)
            for i in range(NT):
                pool.indirect_dma_start(out=sorted_x[:, :], out_offset=bass.IndirectOffsetOnAxis(
                    ap=pos[:, i:i + 1], axis=0), in_=x2[:, i, :], in_offset=None).then_inc(s_scat, 16)
            for u in range(2):
                pool.wait_ge(s_yst[u], 16 * NS // 2)
            for i in range(NT):
                pool.indirect_dma_start(out=yg[:, i, :], out_offset=None, in_=sorted_y[:, :],
                                        in_offset=bass.IndirectOffsetOnAxis(
                                            ap=pos[:, i:i + 1], axis=0)).then_inc(s_gath, 16)

        N_CONST = 16
        H = NT // 2

        @block.vector
        def _(v):
            chain = [0]

            def link(ins):
                chain[0] += 1
                ins.then_inc(s_dve, 1)
                v.wait_ge(s_dve, chain[0])

            v.wait_ge(s_const, N_CONST)
            v.wait_ge(s_small, 1)
            v.tensor_copy(smallT[:], bank[0][:, 0:24]).then_inc(s_smallc, 1)
            v.tensor_copy(U_sb[:], bank[1][:, 0:P]).then_inc(s_smallc, 1)
            v.tensor_copy(ovC[:, 0:P], bank[2][:, 0:P]).then_inc(s_smallc, 1)
            v.tensor_copy(ovC[:, P:P + 1], ident[:, LAST:P]).then_inc(s_smallc, 1)
            v.wait_ge(s_small, 2)
            link(v.tensor_scalar(G_hi[:], bank[3][:, 0:P], QK_SCALE, None, ALU.mult))
            link(v.tensor_scalar(cent_hi[:], bank[4][:, 0:E], QK_SCALE, None, ALU.mult))
            v.scalar_tensor_tensor(out=G_lo[:], in0=bank[3][:, 0:P], scalar=QK_SCALE, in1=G_hi[:],
                                   op0=ALU.mult, op1=ALU.subtract).then_inc(s_smallc, 1)
            v.scalar_tensor_tensor(out=cent_lo[:], in0=bank[4][:, 0:E], scalar=QK_SCALE, in1=cent_hi[:],
                                   op0=ALU.mult, op1=ALU.subtract).then_inc(s_smallc, 1)
            link(v.tensor_scalar(b2_hi[:], b2_sb[:], W_SCALE, None, ALU.mult))
            link(v.scalar_tensor_tensor(out=b2_lo[:], in0=b2_sb[:], scalar=W_SCALE, in1=b2_hi[:],
                                        op0=ALU.mult, op1=ALU.subtract))
            link(v.tensor_copy(b2_hl[:], b2_lo[:]))
            v.tensor_copy(b2_hl[0:1, :], b2_hi[0:1, :]).then_inc(s_smallc, 1)

            def stats_half(h):
                for g in range(h * NG // 2, (h + 1) * NG // 2):
                    v.wait_ge(s_xin[g], 16)
                    for i in range(g * GT, (g + 1) * GT):
                        link(v.bn_stats(stats[:, i % 2, :], x_sb[:, i, :]))
                        ins = v.bn_aggr(mv[:, i, :], stats[:, i % 2, :])
                link(ins)
                a = slice(h * H, (h + 1) * H)
                var = mv[:, a, 1:2].rearrange("p a b -> p (a b)")
                link(v.tensor_scalar(vs[:, 0, 0, a], var, EPS, None, ALU.add))
                link(v.reciprocal(nw[:, 0, 0, a], vs[:, 0, 0, a]))
                link(v.tensor_tensor(nw[:, 0, 1, a], nw[:, 0, 0, a], var, ALU.mult))
                link(v.tensor_scalar(vs[:, 0, 1, a], nw[:, 0, 1, a], EPS, None, ALU.add))
                v.sem_inc(s_dve_roots, 1)
                v.wait_ge(s_actc, h + 1)
                link(v.reciprocal(rs[:, :, a], vs[:, 1, :, a]))
                link(v.tensor_tensor(nw[:, 0, :, a], rs[:, :, a], rs[:, :, a], ALU.mult))
                link(v.tensor_tensor(nw[:, 1, :, a], nw[:, 0, :, a], vs[:, 0, :, a], ALU.mult))
                link(v.tensor_scalar(nw[:, 0, :, a], nw[:, 1, :, a], -0.5, 1.5, ALU.mult, ALU.add))
                link(v.tensor_tensor(rs[:, :, a], rs[:, :, a], nw[:, 0, :, a], ALU.mult))

            def normalise_half(h):
                with v.Fori(h * H, (h + 1) * H) as i:
                    v.tensor_scalar(tile(xn, i), tile(x_sb, i), tile(mv, i)[:, 0:1],
                                    rs[:, 0, bass.ds(i, 1)], ALU.subtract, ALU.mult).then_inc(s_xa, 1)
                with v.Fori(h * NG // 2, (h + 1) * NG // 2) as g:
                    v.wait_ge(s_xahi, g + 1)
                    v.tensor_tensor(tile(lo_g, g, GW), tile(xn_g, g, GW), tile(hi_g, g, GW), ALU.subtract).then_inc(s_xalo, 1)
                a = slice(h * H, (h + 1) * H)
                v.wait_ge(s_xalo, (h + 1) * NG // 2)
                v.memset(xa_hi[:, a, LAST:P], 1.0).then_inc(s_aug, 1)
                v.memset(xa_lo[:, a, LAST:P], 0.0).then_inc(s_aug, 1)
                with v.Fori(h * H, (h + 1) * H) as i:
                    v.wait_ge(s_x2hi, i + 1)
                    v.scalar_tensor_tensor(out=tile(x2, i)[:, P:2 * P], in0=tile(xn, i), scalar=rs[:, 1, bass.ds(i, 1)],
                                           in1=tile(x2, i)[:, 0:P], op0=ALU.mult, op1=ALU.subtract).then_inc(s_x2lo, 1)
                v.wait_ge(s_x2lo, (h + 1) * H)
                link(v.memset(x2[:, a, LAST:P], 1.0))
                link(v.memset(x2[:, a, 2 * P - 1:2 * P], 0.0))

            def low_halves():
                with v.Fori(0, NG // 2) as r:
                    for u in range(2):
                        g = r * 2 + u
                        v.wait_ge(s_khi, g + 1)
                        v.tensor_copy(cols(kT_lo, g), bank[u][:].bitcast(F16)[:, GW:2 * GW]).then_inc(s_klo, 1)
                        v.wait_ge(s_qhi, g + 1)
                        v.scalar_tensor_tensor(out=cols(qT_lo, g), in0=bank[2 + u][:], scalar=1.0 / QK_SCALE, in1=cols(qT_hi, g),
                                               op0=ALU.mult, op1=ALU.subtract).then_inc(s_qlo, 1)

            for h in range(2):
                stats_half(h)
                normalise_half(h)
            low_halves()

            with v.Fori(0, E // 2) as r:
                for u in range(2):
                    e = r * 2 + u
                    v.tensor_scalar(A_e[:, u, :], CT[:], smallT[:, bass.ds(e + 8, 1)], None, ALU.mult).then_inc(s_Aw, 1)
                    v.wait_ge(s_Aw, e + 1)
                    v.tensor_copy(A_e[:, u, LAST:P], smallT[:, bass.ds(e + 16, 1)]).then_inc(s_Ae, 1)
                    v.wait_ge(s_w2hi, e + 1)
                    v.scalar_tensor_tensor(out=tile(w2_hl, e)[:, F:2 * F], in0=w_raw[:, 1, :], scalar=W_SCALE, in1=tile(w2_hl, e)[:, 0:F],
                                           op0=ALU.mult, op1=ALU.subtract).then_inc(s_w2lo, 1)
                    v.wait_ge(s_w1hi, e + 1)
                    v.scalar_tensor_tensor(out=tile(w1_hl, e)[:, F:2 * F], in0=bank[5 + u][:], scalar=W_SCALE, in1=tile(w1_hl, e)[:, 0:F],
                                           op0=ALU.mult, op1=ALU.subtract).then_inc(s_w1lo, 1)

            v.wait_ge(s_affp, NG)
            link(v.tensor_copy(flat(aff[:]), bank[4][:, 0:NT * E]))
            v.tensor_reduce(amax[:], aff[:], AX.X, ALU.max).then_inc(s_amax, 1)
            v.wait_ge(s_amax, 1)
            wide = [P, NT, E]
            link(v.tensor_tensor(hit[:], aff[:], amax[:, :].unsqueeze(2).broadcast_to(wide), ALU.is_equal))
            link(v.tensor_tensor(hit[:], hit[:], rank_w[:, :].unsqueeze(1).broadcast_to(wide), ALU.mult))
            link(v.tensor_reduce(posf[:], hit[:], AX.X, ALU.max))
            link(v.tensor_tensor(onehot[:], hit[:], posf[:, :].unsqueeze(2).broadcast_to(wide), ALU.is_equal))
            v.tensor_copy(onehot16[:], onehot[:]).then_inc(s_onehot, 1)
            v.wait_ge(s_cnt, 1)
            link(v.tensor_copy(flat(cum[:, 0, :, :]), bank[6][:, 0:NT * E]))
            link(v.tensor_copy(below[:], bank[5][:, 0:NT * E].rearrange("p (t e) -> p t e", e=E)))
            src, step = 0, 1
            while step < NT:
                v.tensor_copy(cum[:, 1 - src, 0:step, :], cum[:, src, 0:step, :])
                link(v.tensor_tensor(cum[:, 1 - src, step:, :], cum[:, src, step:, :], cum[:, src, 0:NT - step, :], ALU.add))
                src, step = 1 - src, 2 * step
            link(v.tensor_scalar(cnt_i[:], cum[:, src, NT - 1, :], float(FW - 1), None, ALU.add))
            link(v.tensor_tensor(below[:, 1:, :], below[:, 1:, :], cum[:, src, 0:NT - 1, :], ALU.add))
            link(v.tensor_scalar(tiles_i[:], cnt_i[:], FW.bit_length() - 1, None, ALU.arith_shift_right))
            link(v.tensor_copy(tcum[:, 0, :], tiles_i[:]))
            link(v.tensor_copy(tiles_f[:], tiles_i[:]))
            src, step = 0, 1
            while step < E:
                v.tensor_copy(tcum[:, 1 - src, 0:step], tcum[:, src, 0:step])
                link(v.tensor_tensor(tcum[:, 1 - src, step:], tcum[:, src, step:], tcum[:, src, 0:E - step], ALU.add))
                src, step = 1 - src, 2 * step
            link(v.tensor_tensor(base[:], tcum[:, src, :], tiles_f[:], ALU.subtract))
            link(v.tensor_tensor(slot_hit[:], slot[:], base[0:1, :].unsqueeze(1).broadcast_to([1, NS, E]), ALU.is_ge))
            link(v.tensor_reduce(tile_ef[:], slot_hit[:], AX.X, ALU.add))
            v.tensor_scalar(tile_e[:, 0:NS], tile_ef[:], -1.0, None, ALU.add).then_inc(s_tile_e, 1)
            link(v.tensor_scalar(base[:], base[:], float(FW), None, ALU.mult))
            link(v.tensor_tensor(below[:], below[:], base[:, :].unsqueeze(1).broadcast_to(wide), ALU.add))
            link(v.tensor_tensor(below[:], below[:], onehot[:], ALU.mult))
            link(v.tensor_reduce(posf[:], below[:], AX.X, ALU.add))
            link(v.tensor_copy(pos[:], posf[:]))
            v.sem_inc(s_pos, 1)
            v.wait_ge(s_actc, 3)
            link(v.tensor_scalar(eneg[:], eneg[:], 1.0, None, ALU.add))
            link(v.reciprocal(alpha[:], eneg[:]))

            def reduce_unit(n, par, i, c, width, wait_extra=None):
                v.wait_ge(s_max_mm, n + 1)
                v.tensor_reduce(row_max[:, i, c:c + 1] if isinstance(c, int) else row_max[:, i, bass.ds(c, 1)],
                                bank[2 + par][:, 0:width], AX.X, ALU.max).then_inc(s_max, 1)

            def shift(b, g, units_done, nth):
                v.wait_ge(s_max, units_done)
                if g:
                    link(v.tensor_reduce(row_m[:], row_max[:, :, 0:g + 1], AX.X, ALU.max))
                    m = row_m[:]
                else:
                    m = row_max[:, :, 0]
                v.tensor_scalar(neg_max[:, :, LAST], m, -1.0, SHIFT, ALU.mult, ALU.add).then_inc(s_neg, 1)
                v.wait_ge(s_negT, nth + 1)
                q = qT_hi[96:P, (b * BG + g) * GW:(b * BG + g + 1) * GW]
                v.tensor_tensor(q, q, bank[5][96:P, :], ALU.add).then_inc(s_shift, 1)

            def weights_low(n, par, off):
                v.wait_ge(s_exp, n + 1)
                wait(v, s_pvlo, n - 1)
                v.tensor_tensor(p_lo[:, par, off:GW], p_sb[:, par, off:GW], p_hi[:, par, off:GW],
                                ALU.subtract).then_inc(s_plo, 1)

            def attention(b):
                n0 = b * STEPS
                for i in range(GT):
                    reduce_unit(n0 + i, i % 2, i, 0, (i + 1) * P)
                shift(b, 0, n0 + GT, b * BG)
                u0 = n0 + GT
                for g in range(BG):
                    more = g + 1 < BG
                    if g:
                        with v.Fori(0, g) as c:
                            for i in range(GT):
                                if more:
                                    reduce_unit(c * GT + (u0 + i), i % 2, i, c, GW)
                                weights_low(c * GT + (n0 + i), i % 2, 0)
                    for i in range(GT):
                        if more:
                            reduce_unit(u0 + g * GT + i, i % 2, i, g, GW)
                        weights_low(n0 + g * GT + i, i % 2, i * P)
                    if more:
                        for i in range(GT):
                            reduce_unit(u0 + (g + 1) * GT + i, i % 2, i, g + 1, (i + 1) * P)
                        u0 += GT * (g + 2)
                        shift(b, g + 1, u0, b * BG + g + 1)
                    n0 += GT * (g + 1)
                    for f in range(2):
                        n = (b * BG + g) * 2 + f
                        v.wait_ge(s_fin, n + 1)
                        o = bank[6 + f][:, 0:2 * (P + 1)].rearrange("p (t d) -> p t d", t=2)
                        wait(v, s_att, n - 1)
                        link(v.reciprocal(inv_den[:, f, :], o[:, :, P]))
                        for t in range(2):
                            dst = x_sb[:, (b * BG + g) * GT + f * 2 + t, :]
                            ins = v.scalar_tensor_tensor(out=dst, in0=o[:, t, 0:P], scalar=inv_den[:, f, t:t + 1], in1=dst,
                                                         op0=ALU.mult, op1=ALU.add)
                        ins.then_inc(s_att, 1)

            def ffn():
                def lows(k, u):
                    v.wait_ge(s_hhi, k + 1)
                    v.scalar_tensor_tensor(out=h_lo[:, u, :], in0=hidden_ps[u], scalar=0.0, in1=h_hi[:, u, :],
                                           op0=ALU.max, op1=ALU.subtract).then_inc(s_hlo, 1)

                def turned(k, u):
                    v.wait_ge(s_tr, k + 1)
                    v.tensor_copy(x2T[:, u, :], bank[6 + u][:].bitcast(F16)[:, 0:2 * FW]).then_inc(s_x2T, 1)

                turned(0, 0)
                turned(1, 1)
                lows(0, 0)
                turned(2, 0)
                lows(1, 1)
                turned(3, 1)
                with v.Fori(1, NS // 2 - 1) as r:
                    for u in range(2):
                        lows(r * 2 + u, u)
                        turned(r * 2 + (u + 2), u)
                for u in range(2):
                    lows(NS - 2 + u, u)

            def combine(b):
                for g in range(b * BG, (b + 1) * BG):
                    v.wait_ge(s_gath, 16 * NT) if g == 0 else None
                    v.wait_ge(s_att, 2 * (g + 1))
                    for i in range(g * GT, (g + 1) * GT):
                        ins = v.scalar_tensor_tensor(out=x_sb[:, i, :], in0=yg[:, i, :], scalar=alpha[:, i:i + 1],
                                                     in1=x_sb[:, i, :], op0=ALU.mult, op1=ALU.add)
                    ins.then_inc(s_sum, 1)

            v.wait_ge(s_basep, NG)
            attention(0)
            ffn()
            attention(1)
            combine(0)
            combine(1)

        @block.scalar
        def _(a):
            a.wait_ge(s_const, N_CONST)
            for h in range(2):
                t = slice(h * H, (h + 1) * H)
                a.wait_ge(s_dve_roots, h + 1)
                a.activation(vs[:, 1, :, t], vs[:, 0, :, t], ACT.Sqrt).then_inc(s_actc, 1)
                with a.Fori(h * NG // 2, (h + 1) * NG // 2) as g:
                    a.wait_ge(s_xa, g * GT + GT)
                    a.activation(tile(hi_g, g, GW), tile(xn_g, g, GW), ACT.Copy).then_inc(s_xahi, 1)
                with a.Fori(h * H, (h + 1) * H) as i:
                    a.activation(tile(x2, i)[:, 0:P], tile(xn, i), ACT.Copy, scale=rs[:, 1, bass.ds(i, 1)]).then_inc(s_x2hi, 1)
            with a.Fori(0, NG // 2) as r:
                for u in range(2):
                    g = r * 2 + u
                    a.wait_ge(s_kp, g + 1)
                    a.activation(cols(kT_hi, g), bank[u][:].bitcast(F16)[:, 0:GW], ACT.Copy).then_inc(s_khi, 1)
                    a.wait_ge(s_qp, g + 1)
                    a.activation(cols(qT_hi, g), bank[2 + u][:], ACT.Copy, scale=1.0 / QK_SCALE).then_inc(s_qhi, 1)
            with a.Fori(0, E // 2) as r:
                for u in range(2):
                    e = r * 2 + u
                    a.wait_ge(s_wl[1], e * 16 + 16)
                    a.activation(tile(w2_hl, e)[:, 0:F], w_raw[:, 1, :], ACT.Copy, scale=W_SCALE).then_inc(s_w2hi, 1)
                    a.wait_ge(s_w1p, e + 1)
                    a.activation(tile(w1_hl, e)[:, 0:F], bank[5 + u][:], ACT.Copy, scale=W_SCALE).then_inc(s_w1hi, 1)
            a.wait_ge(s_amax, 1)
            a.activation(eneg[:], amax[:], ACT.Exp, scale=-1.0 / QK_SCALE).then_inc(s_actc, 1)

            def exp_step(n, par, off):
                a.wait_ge(s_sc, n + 1)
                wait(a, s_pv, n - 1)
                wait(a, s_plo, n - 1)
                a.activation(p_hi[:, par, off:GW], bank[par][:, off:GW], ACT.Exp, scale=SCALE).then_inc(s_phi, 1)
                a.activation(p_sb[:, par, off:GW], bank[par][:, off:GW], ACT.Exp, scale=SCALE).then_inc(s_exp, 1)

            def attention(b):
                n0 = b * STEPS
                for g in range(BG):
                    if g:
                        with a.Fori(0, g) as c:
                            for i in range(GT):
                                exp_step(c * GT + (n0 + i), i % 2, 0)
                    for i in range(GT):
                        exp_step(n0 + g * GT + i, i % 2, i * P)
                    n0 += GT * (g + 1)
                    a.wait_ge(s_pvlo, n0)
                    if b * BG + g:
                        a.wait_ge(s_fin, 2 * (b * BG + g))
                    a.activation(oT[:], bank[4][:], ACT.Copy).then_inc(s_oT, 1)

            def ffn():
                def highs(k, u):
                    a.wait_ge(s_z, k + 1)
                    a.activation(h_hi[:, u, :], hidden_ps[u], ACT.Relu).then_inc(s_hhi, 1)

                def rows(k, u):
                    a.wait_ge(s_y, k + 1)
                    if not isinstance(k, int) or k >= 2:
                        a.wait_ge(s_yst[u], (k - u) * 8)
                    a.activation(y_sb[:, u, :], bank[4 + u][:, 0:FT * P], ACT.Copy,
                                 scale=1.0 / (W_SCALE * W_SCALE)).then_inc(s_ysb, 1)

                highs(0, 0)
                for k in range(2):
                    highs(k + 1, (k + 1) % 2)
                    rows(k, k % 2)
                with a.Fori(1, NS // 2 - 1) as r:
                    for u in range(2):
                        highs(r * 2 + (u + 1), 1 - u)
                        rows(r * 2 + u, u)
                highs(NS - 1, 1)
                rows(NS - 2, 0)
                rows(NS - 1, 1)

            attention(0)
            ffn()
            attention(1)

        @block.tensor
        def _(pe):
            pe.wait_ge(s_const, N_CONST)
            pe.wait_ge(s_win, 16 * 8)
            mm = pe.matmul
            pe.transpose(bank[0][:, 0:24], small[:], ident[0:24, 0:24])
            mm(bank[1][:, 0:P], qk_sb[:], CT[:], start=True, stop=True)
            mm(bank[2][:, 0:P], CT[:], ov_sb[:], start=True, stop=True).then_inc(s_small, 1)
            pe.wait_ge(s_smallc, 4)
            mm(bank[4][:, 0:E], CT[:], smallT[:, 0:E], start=True, stop=True)
            mm(bank[3][:, 0:P], U_sb[:], CT[:], start=True, stop=True).then_inc(s_small, 1)
            pe.wait_ge(s_smallc, 7)

            def features(g, u):
                for half, t16 in enumerate((xa_hi, xa_lo)):
                    for i in range(GT):
                        c = half * GW + i * P
                        t = pe.transpose(bank[u][:].bitcast(F16)[:, c:c + P], tile(t16, g * GT + i), ident16[:])
                t.then_inc(s_kp, 1)

            def queries(g, u):
                pe.wait_ge(s_khi, g + 1)
                pe.wait_ge(s_klo, g + 1)
                q = bank[2 + u][:]
                mm(q, G_hi[:], cols(kT_hi, g), start=True, stop=False)
                mm(q, G_hi[:], cols(kT_lo, g), start=False, stop=False)
                mm(q, G_lo[:], cols(kT_hi, g), start=False, stop=True).then_inc(s_qp, 1)
                for i in range(GT):
                    hi, lo = (t[:, bass.ds(g * GW + i * P, P)] for t in (kT_hi, kT_lo))
                    to = bank[4][:, bass.ds(g * (GT * E) + i * E, E)]
                    mm(to, hi, cent_hi[:], start=True, stop=False)
                    mm(to, hi, cent_lo[:], start=False, stop=False)
                    t = mm(to, lo, cent_hi[:], start=False, stop=True)
                t.then_inc(s_affp, 1)

            for h in range(2):
                pe.wait_ge(s_aug, 2 * (h + 1))
                with pe.Fori(h * NG // 4, (h + 1) * NG // 4) as r:
                    for u in range(2):
                        g = r * 2 + u
                        features(g, u)
                        queries(g, u)

            with pe.Fori(0, E // 2) as r:
                for u in range(2):
                    e = r * 2 + u
                    pe.wait_ge(s_Ae, e + 1)
                    pe.wait_ge(s_wl[0], e * 16 + 16)
                    mm(bank[5 + u][:], A_e[:, u, :], w_raw[:, 0, :], start=True, stop=False)
                    mm(bank[5 + u][:], last_row[:], b1_sb[:, bass.ds(e * F, F)], start=False, stop=True).then_inc(s_w1p, 1)
            pe.wait_ge(s_w1lo, E)
            pe.wait_ge(s_onehot, 1)
            oh = onehot16[:].rearrange("p t e -> p (t e)")
            mm(bank[5][:, 0:NT * E], upper[:], oh, start=True, stop=True)
            mm(bank[6][:, 0:NT * E], ones16[:], oh, start=True, stop=True).then_inc(s_cnt, 1)

            def max_unit(n, b, g, par, i, c, width):
                wait(pe, s_max, n - 1)
                q = (b * BG + g) * GW + i * P
                diag = width is not None
                w = width or GW
                dst = bank[2 + par][:, 0:w]
                first = mm(dst, qT_hi[:, q:q + P], kT_hi[:, bass.ds(c * GW + b * S, w)], start=True, stop=not diag)
                if diag:
                    mm(bank[2 + par][:, w - P:w], ident16[:], mask_qk[:], start=False, stop=True).then_inc(s_max_mm, 1)
                else:
                    pe_last[0].then_inc(s_max_mm, 1)

            pe_last = [None]

            def mmk(*args, **kw):
                pe_last[0] = pe.matmul(*args, **kw)
                return pe_last[0]

            mm = mmk

            def shift(b, g):
                nth = b * BG + g
                pe.wait_ge(s_neg, nth + 1)
                for i in range(GT):
                    t = mm(bank[5][:, i * P:(i + 1) * P], neg_max[:, i, :], ident16[:], start=True, stop=True)
                t.then_inc(s_negT, 1)

            def scores(n, b, g, par, j, off):
                wait(pe, s_exp, n - 1)
                q = slice((b * BG + g) * GW + off, (b * BG + g + 1) * GW)
                k = bass.ds(j * P + b * S, P) if not isinstance(j, int) else slice(b * S + j * P, b * S + (j + 1) * P)
                dst = bank[par][:, off:GW]
                mm(dst, kT_hi[:, k], qT_hi[:, q], start=True, stop=False)
                mm(dst, kT_hi[:, k], qT_lo[:, q], start=False, stop=False)
                diag = isinstance(j, int) and j >= g * GT
                mm(dst, kT_lo[:, k], qT_hi[:, q], start=False, stop=not diag)
                if diag:
                    mm(bank[par][:, off:off + P], ident16[:], mask_kq[:], start=False, stop=True)
                pe_last[0].then_inc(s_sc, 1)

            def rows(t, b, j):
                return tile(t, j + b * BT)

            def weighted(n, b, g, par, j, off):
                first = isinstance(j, int) and j == 0
                if first:
                    wait(pe, s_oT, b * BG + g)
                pe.wait_ge(s_phi, n + 1)
                to, w = bank[4][:, off:GW], p_hi[:, par, off:GW]
                mm(to, rows(xa_hi, b, j), w, start=first, stop=False, skip_group_check=True)
                mm(to, rows(xa_lo, b, j), w, start=False, stop=False, skip_group_check=True).then_inc(s_pv, 1)

            def weighted_low(n, b, g, par, j, off):
                pe.wait_ge(s_plo, n + 1)
                last = isinstance(j, int) and j == g * GT + GT - 1
                mm(bank[4][:, off:GW], rows(xa_hi, b, j), p_lo[:, par, off:GW], start=False, stop=last,
                   skip_group_check=True).then_inc(s_pvlo, 1)

            def project(b, g):
                nth = b * BG + g
                pe.wait_ge(s_oT, nth + 1)
                if nth:
                    pe.wait_ge(s_att, 2 * nth)
                for f in range(2):
                    for t in range(2):
                        i = f * 2 + t
                        m = mm(bank[6 + f][:, t * (P + 1):(t + 1) * (P + 1)], oT[:, i * P:(i + 1) * P], ovC[:],
                               start=True, stop=True)
                    m.then_inc(s_fin, 1)

            def attention(b):
                n0 = b * STEPS
                for i in range(GT):
                    max_unit(n0 + i, b, 0, i % 2, i, 0, (i + 1) * P)
                shift(b, 0)
                u0 = n0 + GT
                for g in range(BG):
                    more = g + 1 < BG
                    diag = g * GT

                    def step(c, i, first=False):
                        j = c * GT + i
                        on = isinstance(c, int) and c == g
                        if not (on and i == GT - 1):
                            scores(j + (n0 + 1), b, g, (i + 1) % 2, j + 1, (i + 1) * P if on else 0)
                        if more:
                            max_unit(j + u0, b, g + 1, i % 2, i, c, None)
                        if not first:
                            weighted_low(j + (n0 - 1), b, g, (i + 1) % 2, j - 1, (i - 1) * P if on and i else 0)
                        weighted(j + n0, b, g, i % 2, j, i * P if on else 0)

                    pe.wait_ge(s_shift, b * BG + g + 1)
                    scores(n0, b, g, 0, 0, 0)
                    for i in range(GT - 1 if g else GT):
                        step(0, i, first=(i == 0))
                    if g > 1:
                        with pe.Fori(1, g) as c:
                            step(c - 1, GT - 1)
                            for i in range(GT - 1):
                                step(c, i)
                    if g:
                        step(g - 1, GT - 1)
                        for i in range(GT):
                            step(g, i)
                    weighted_low(n0 + diag + GT - 1, b, g, 1, diag + GT - 1, (GT - 1) * P)
                    if more:
                        for i in range(GT):
                            max_unit(u0 + diag + GT + i, b, g + 1, i % 2, i, g + 1, (i + 1) * P)
                        shift(b, g + 1)
                        u0 += GT * (g + 2)
                    n0 += GT * (g + 1)
                    project(b, g)

            def ffn():
                pe.wait_ge(s_tile_e, 1)

                def turn(k, u):
                    wait(pe, s_x2T, k - 1)
                    pe.wait_ge(s_xs[u], (k - u) * 8 + 16)
                    for half in range(2):
                        for t in range(FT):
                            m = pe.transpose(bank[6 + u][:].bitcast(F16)[:, half * FW + t * P:half * FW + (t + 1) * P],
                                             xs_sb[:, u, t, half * P:(half + 1) * P], ident16[:])
                    m.then_inc(s_tr, 1)

                def hidden(k, u, e):
                    pe.wait_ge(s_x2T, k + 1)
                    wait(pe, s_hlo, k - 1)
                    for c in range(FC):
                        dst = hidden_ps[u][:, c * FW:(c + 1) * FW]
                        hi = w1_flat[:, bass.ds(e * (2 * F) + c * P, P)]
                        lo = w1_flat[:, bass.ds(e * (2 * F) + (F + c * P), P)]
                        mm(dst, hi, x2T[:, u, 0:FW], start=True, stop=False)
                        mm(dst, hi, x2T[:, u, FW:2 * FW], start=False, stop=False)
                        m = mm(dst, lo, x2T[:, u, 0:FW], start=False, stop=True)
                    m.then_inc(s_z, 1)

                def output(k, u, e):
                    wait(pe, s_ysb, k - 1)
                    pe.wait_ge(s_hlo, k + 1)
                    to = [bank[4 + u][:, t * P:(t + 1) * P] for t in range(FT)]
                    for t in range(FT):
                        mm(to[t], row16[:], b2_hl[:, bass.ds(e * P, P)], start=(t == 0), stop=False, skip_group_check=True)
                    for c in range(FC):
                        hi = w2_flat[:, bass.ds(e * (2 * F) + c * P, P)]
                        lo = w2_flat[:, bass.ds(e * (2 * F) + (F + c * P), P)]
                        for t in range(FT):
                            at = slice(c * FW + t * P, c * FW + (t + 1) * P)
                            mm(to[t], h_hi[:, u, at], hi, start=False, stop=False, skip_group_check=True)
                            mm(to[t], h_hi[:, u, at], lo, start=False, stop=False, skip_group_check=True)
                            m = mm(to[t], h_lo[:, u, at], hi, start=False, stop=(c == FC - 1), skip_group_check=True)
                    m.then_inc(s_y, 1)

                def experts(k, n=4):
                    _, values = nc.values_load_multi_w_load_instructions(
                        tile_e[0:1, bass.ds(k, n)], engines=[mybir.EngineType.PE], min_val=0, max_val=E - 1,
                        skip_runtime_bounds_check_because="a count of at most E experts, less one")
                    return values

                def round2(k, last=False):
                    e = experts(k)
                    for u in range(2):
                        output(k + u, u, e[u])
                        if not (isinstance(k, int) and k + u + 2 >= NS):
                            hidden(k + u + 2, u, e[u + 2])
                        if not (isinstance(k, int) and k + u + 3 >= NS):
                            turn(k + u + 3, 1 - u)

                turn(0, 0)
                turn(1, 1)
                e = experts(0)
                hidden(0, 0, e[0])
                turn(2, 0)
                hidden(1, 1, e[1])
                round2(0)
                with pe.Fori(1, NS // 2 - 2) as r:
                    round2(r * 2)
                round2(NS - 4)
                round2(NS - 2)

            attention(0)
            pe.wait_ge(s_exp, STEPS)
            pe.wait_ge(s_max, STEPS)
            pe.wait_ge(s_att, 2 * BG)
            ffn()
            pe.wait_ge(s_hlo, NS)
            pe.wait_ge(s_ysb, NS)
            attention(1)


_INS = ['L0_attn_input_data', 'L0_attn_qk', 'L0_attn_ov', 'L0_ffn_centroids', 'L0_ffn_ln_g', 'L0_ffn_ln_b',
        'L0_ffn_w1', 'L0_ffn_b1', 'L0_ffn_w2', 'L0_ffn_b2']


def kernel(**inputs):
    import numpy as _np
    import concourse.bacc as _bacc
    from concourse import mybir as _mybir
    from concourse.bass_utils import run_bass_kernel_spmd as _run

    nc = _bacc.Bacc("TRN2", target_bir_lowering=False, num_devices=1)
    arrays, args = {}, []
    for name in _INS:
        a = _np.ascontiguousarray(inputs[name])
        arrays[f"in_{name}"] = a
        args.append(nc.dram_tensor(f"in_{name}", a.shape, _mybir.dt.from_np(a.dtype), kind="ExternalInput").ap())
    B, S, D = inputs['L0_attn_input_data'].shape
    E = inputs['L0_ffn_w1'].shape[0]
    rows = B * S + E * 256
    args.append(nc.dram_tensor("sorted_x", (rows, 2 * D), _mybir.dt.float16, kind="Internal").ap())
    args.append(nc.dram_tensor("sorted_y", (rows, D), _mybir.dt.float32, kind="Internal").ap())
    args.append(nc.dram_tensor("out", (B, S, D), _mybir.dt.float32, kind="ExternalOutput").ap())
    build(nc, *args)
    r = _run(nc, [arrays], core_ids=[0])
    return r.results[0]["out"]
```

```python
import concourse.bass as bass
from concourse import mybir
from contextlib import ExitStack

F32 = mybir.dt.float32
F16 = mybir.dt.float16
BF16 = mybir.dt.bfloat16
I32 = mybir.dt.int32
U32 = mybir.dt.uint32
ALU = mybir.AluOpType
ACT = mybir.ActivationFunctionType
AX = mybir.AxisListType

P = 128
EPS = 1e-5
W_SCALE = 16.0
QK_SCALE = 64.0
SHIFT = 32.0
MASK = -1e30
LAST = P - 1


def flat(ap):
    return ap.rearrange("p a b -> p (a b)")


def build(nc, x, qk, ov, cent, ln_g, ln_b, w1, b1, w2, b2, sorted_x, sorted_y, out):
    B, S, D = x.shape
    E, _, F = w1.shape
    assert D == P
    N = B * S
    NT = N // P
    GT = 4
    GW = GT * P
    NG = N // GW
    BG = S // GW
    BT = S // P
    FC = F // P
    FT = 2
    FW = FT * P
    NS = NT // FT + E
    UNITS = [GT * (g + 1) for g in range(BG)]
    STEPS = sum(UNITS)
    SCALE = float(D) ** -0.5

    x_t = x.rearrange("b (t p) d -> p (b t) d", p=P)
    out_t = out.rearrange("b (t p) d -> p (b t) d", p=P)

    with ExitStack() as ctx:
        def sb(name, shape, dt=F32):
            return ctx.enter_context(nc.sbuf_tensor(name, shape, dt))

        def sem(name):
            return ctx.enter_context(nc.semaphore(name))

        x_sb = sb("x_sb", [P, NT, P])
        xn = sb("xn", [P, NT, P])
        yg = xn
        xa_hi = sb("xa_hi", [P, NT, P], F16)
        xa_lo = sb("xa_lo", [P, NT, P], F16)
        x2 = sb("x2", [P, NT, 2 * P], F16)
        kT_hi = sb("kT_hi", [P, N], F16)
        kT_lo = sb("kT_lo", [P, N], F16)
        qT_hi = sb("qT_hi", [P, N], F16)
        qT_lo = sb("qT_lo", [P, N], F16)
        w1_raw = sb("w1_raw", [P, 2, F])
        w2_raw = sb("w2_raw", [P, 2, F])
        b1_raw = sb("b1_raw", [1, 2, F])
        x2_f = sb("x2_f", [P, 2, GT, P])
        w1_hl = sb("w1_hl", [P, E, 2 * F], F16)
        w2_hl = sb("w2_hl", [P, E, 2 * F], F16)
        b2_sb = sb("b2_sb", [2, E * P])
        b2_hi = sb("b2_hi", [2, E * P], F16)
        b2_lo = sb("b2_lo", [2, E * P])
        b2_hl = sb("b2_hl", [2, E * P], F16)
        small = sb("small", [3 * 8, P])
        smallT = sb("smallT", [P, 3 * 8])
        cent_hi = sb("cent_hi", [P, E], F16)
        cent_lo = sb("cent_lo", [P, E], F16)
        qk_sb = sb("qk_sb", [P, P])
        ov_sb = sb("ov_sb", [P, P])
        ovC = sb("ovC", [P, P + 1])
        U_sb = sb("U_sb", [P, P])
        G_hi = sb("G_hi", [P, P], F16)
        G_lo = sb("G_lo", [P, P], F16)
        A_e = sb("A_e", [P, 2, P])
        ident = sb("ident", [P, P])
        ident16 = sb("ident16", [P, P], F16)
        CT = sb("CT", [P, P])
        onesf = sb("onesf", [P, P])
        ones16 = sb("ones16", [P, P], F16)
        upper = sb("upper", [P, P], F16)
        mask_qk = sb("mask_qk", [P, P], BF16)
        mask_kq = sb("mask_kq", [P, P], BF16)
        stats = sb("stats", [P, NT, 6])
        mv = sb("mv", [P, NT, 2])
        vs = sb("vs", [P, 2, 2, NT])
        rs = sb("rs", [P, 2, NT])
        nw = sb("nw", [P, 2, 2, NT])
        aff = sb("aff", [P, NT, E])
        amax = sb("amax", [P, NT])
        eneg = sb("eneg", [P, NT])
        alpha = sb("alpha", [P, NT])
        hit = sb("hit", [P, NT, E])
        rank_w = sb("rank_w", [P, E])
        onehot = sb("onehot", [P, NT, E])
        onehot16 = sb("onehot16", [P, NT, E], F16)
        cum = sb("cum", [P, 2, NT, E])
        below = sb("below", [P, NT, E])
        cnt = sb("cnt", [P, E])
        cnt_i = sb("cnt_i", [P, E], I32)
        tiles_i = sb("tiles_i", [P, E], I32)
        tiles_f = sb("tiles_f", [P, E])
        tcum = sb("tcum", [P, 2, E])
        base = sb("base", [P, E])
        posf = sb("posf", [P, NT])
        pos = sb("pos", [P, NT], U32)
        slot = sb("slot", [1, NS, E])
        slot_hit = sb("slot_hit", [1, NS, E])
        tile_ef = sb("tile_ef", [1, NS])
        tile_e = sb("tile_e", [1, NS + 4], I32)
        zero = sb("zero", [P, 2 * P], F16)
        row_max = sb("row_max", [P, GT, BG])
        row_m = sb("row_m", [P, GT])
        neg_max = sb("neg_max", [P, GT, P], F16)
        p_sb = sb("p_sb", [P, 2, GW])
        p_hi = sb("p_hi", [P, 2, GW], F16)
        p_lo = sb("p_lo", [P, 2, GW], F16)
        oT = sb("oT", [P, GW])
        inv_den = sb("inv_den", [P, 2, 2])
        xs_sb = sb("xs_sb", [P, 2, FT, 2 * P], F16)
        x2T = sb("x2T", [P, 2, 2 * FW], F16)
        h_hi = sb("h_hi", [P, 2, FC * FW], F16)
        h_lo = sb("h_lo", [P, 2, FC * FW], F16)
        y_sb = sb("y_sb", [P, 2, FT * P])
        row16 = sb("row16", [2, P], F16)
        last_row = sb("last_row", [1, P])

        psum = ctx.enter_context(nc.psum_tensor("psum", [P, 8, 512], F32))
        bank = [psum[:, i, :] for i in range(8)]

        s_xin = [sem(f"s_xin{i}") for i in range(2)]
        s_bn = sem("s_bn")
        s_ag = sem("s_ag")
        s_centred = sem("s_centred")
        s_x2f = sem("s_x2f")
        s_sum_last = sem("s_sum_last")
        s_win = sem("s_win")
        s_wl = [[sem(f"s_wl{i}{u}") for u in range(2)] for i in range(3)]
        s_const = sem("s_const")
        s_dve = sem("s_dve")
        s_actc = sem("s_actc")
        s_small = sem("s_small")
        s_smallc = sem("s_smallc")
        s_xa = sem("s_xa")
        s_basep = sem("s_basep")
        s_x2hi = sem("s_x2hi")
        s_xahi = sem("s_xahi")
        s_xalo = sem("s_xalo")
        s_kp = sem("s_kp")
        s_khi = sem("s_khi")
        s_klo = sem("s_klo")
        s_phi = sem("s_phi")
        s_plo = sem("s_plo")
        s_pvlo = sem("s_pvlo")
        s_qp = sem("s_qp")
        s_qhi = sem("s_qhi")
        s_qlo = sem("s_qlo")
        s_affp = sem("s_affp")
        s_Ae = sem("s_Ae")
        s_w1p = sem("s_w1p")
        s_w1hi = sem("s_w1hi")
        s_w1lo = sem("s_w1lo")
        s_w2hi = sem("s_w2hi")
        s_w2lo = sem("s_w2lo")
        s_cnt = sem("s_cnt")
        s_onehot = sem("s_onehot")
        s_pos = sem("s_pos")
        s_tile_e = sem("s_tile_e")
        s_zero = sem("s_zero")
        s_zeroed = sem("s_zeroed")
        s_scat = sem("s_scat")
        s_max_mm = sem("s_max_mm")
        s_max = sem("s_max")
        s_neg = sem("s_neg")
        s_negT = sem("s_negT")
        s_shift = sem("s_shift")
        s_sc = sem("s_sc")
        s_exp = sem("s_exp")
        s_pv = sem("s_pv")
        s_oT = sem("s_oT")
        s_fin = sem("s_fin")
        s_att = sem("s_att")
        s_xs = [sem(f"s_xs{i}") for i in range(2)]
        s_tr = sem("s_tr")
        s_x2T = sem("s_x2T")
        s_z = sem("s_z")
        s_hhi = sem("s_hhi")
        s_hlo = sem("s_hlo")
        s_y = sem("s_y")
        s_ysb = sem("s_ysb")
        s_yst = [sem(f"s_yst{i}") for i in range(2)]
        s_gath = sem("s_gath")
        s_sum = sem("s_sum")
        s_out = sem("s_out")
        s_yal = sem("s_yal")
        s_halves = sem("s_halves")
        s_b2hi = sem("s_b2hi")
        s_b2 = sem("s_b2")
        s_dve_roots = sem("s_dve_roots")
        s_x2lo = sem("s_x2lo")
        s_Aw = sem("s_Aw")
        s_amax = sem("s_amax")

        def tile(t, i, n=P):
            return flat(t[:, bass.ds(i, 1), :])

        def most(t, g):
            return t[:, bass.ds(g * GT, GT), 0:LAST]

        xn_g, hi_g, lo_g, x_g = (t[:].rearrange("p (g t) d -> p g (t d)", t=GT) for t in (xn, xa_hi, xa_lo, x_sb))

        w1_flat, w2_flat = (flat(t[:]) for t in (w1_hl, w2_hl))
        hidden_ps = [psum[:, 2 * u:2 * u + 2, :].rearrange("p a b -> p (a b)") for u in range(2)]

        def cols(t, i, n=GW):
            return t[:, bass.ds(i * n, n)]

        def wait(eng, s, n):
            if not isinstance(n, int) or n > 0:
                eng.wait_ge(s, n)

        LAGS = 4

        class Tick:

            def __init__(self, reg, n):
                self.reg, self.n = reg, n

            def __add__(self, k):
                return Tick(self.reg, self.n + k)

            def __sub__(self, k):
                return Tick(self.reg, self.n - k)

        def of(t):
            return t.n if isinstance(t.reg, int) else t.reg + t.n

        def par(t):
            return t.n % 2

        def is_in(t):
            return not isinstance(t.reg, int) or 0 <= t.n < NG

        def ticks(eng, tick):
            for n in range(LAGS):
                tick(Tick(0, n))
            with eng.Fori(LAGS // 2, NG // 2) as r:
                for u in range(2):
                    tick(Tick(r * 2, u))
            for n in range(NG, NG + LAGS + 1):
                tick(Tick(0, n))

        block = ctx.enter_context(nc.Block())

        @block.sync
        def _(sp):
            for g in range(NG):
                sp.dma_start(x_sb[:, g * GT:(g + 1) * GT, :], x_t[:, g * GT:(g + 1) * GT, :]).then_inc(s_xin[g * 2 // NG], 16)
            for e in range(E):
                u = e % 2
                wait(sp, s_w1p, e - 1)
                sp.dma_start(w1_raw[:, u, :], w1[e, :, :]).then_inc(s_wl[0][u], 16)
                sp.dma_start(b1_raw[:, u, :], b1[e:e + 1, :]).then_inc(s_wl[2][u], 16)
                wait(sp, s_w2hi, e - 1)
                wait(sp, s_w2lo, e - 1)
                sp.dma_start(w2_raw[:, u, :].rearrange("p (c d) -> p c d", d=P),
                             w2[e, :, :].rearrange("(c p) d -> p c d", p=P)).then_inc(s_wl[1][u], 16)
            sp.wait_ge(s_zero, 1)
            sp.dma_start(sorted_x.rearrange("(p a) d -> p a d", p=P),
                         zero[:, :].unsqueeze(1).broadcast_to([P, NS * FT, 2 * P])).then_inc(s_zeroed, 16)
            sp.wait_ge(s_scat, 16 * NT)
            src = sorted_x.rearrange("(k t p) d -> k p t d", p=P, t=FT)
            dst = sorted_y.rearrange("(k t p) d -> k p t d", p=P, t=FT)

            def block_of(t, k):
                return (t[bass.ds(k, 1), :, :, :]).rearrange("k p t d -> p (k t) d")

            def load_sorted(k, u):
                sp.dma_start(xs_sb[:, u, :, :], block_of(src, k)).then_inc(s_xs[u], 16)

            def store_sorted(k, u):
                sp.wait_ge(s_ysb, k + 1)
                sp.dma_start(block_of(dst, k), y_sb[:, u, :].rearrange("p (t d) -> p t d", d=P)).then_inc(s_yst[u], 16)

            def move(k, u):
                if not isinstance(k, int) or k < NS:
                    wait(sp, s_tr, k - 1)
                    load_sorted(k, u)
                if not isinstance(k, int) or k >= 4:
                    store_sorted(k - 4, u)

            for k in range(4):
                move(k, k % 2)
            with sp.Fori(2, NS // 2) as r:
                for u in range(2):
                    move(r * 2 + u, u)
            for k in range(NS, NS + 4):
                move(k, k % 2)
            for g in range(NG):
                if g < NG - 1:
                    sp.wait_ge(s_sum, g + 1)
                else:
                    sp.wait_ge(s_sum_last, 1)
                sp.dma_start(out_t[:, g * GT:(g + 1) * GT, :], x_sb[:, g * GT:(g + 1) * GT, :]).then_inc(s_out, 16)
            sp.wait_ge(s_out, 16 * NG)

        @block.gpsimd
        def _(pool):
            pool.memset(zero[:], 0.0).then_inc(s_zero, 1)
            pool.memset(onesf[:], 1.0).then_inc(s_const, 1)
            for dst, value in ((xa_hi[:, :, LAST:P], 1.0), (xa_lo[:, :, LAST:P], 0.0),
                               (x2[:, :, LAST:P], 1.0), (x2[:, :, 2 * P - 1:2 * P], 0.0)):
                pool.memset(dst, value).then_inc(s_const, 1)
            pool.memset(CT[:], 0.0).then_inc(s_const, 1)
            pool.memset(neg_max[:], 0.0).then_inc(s_const, 1)
            pool.memset(row16[:], W_SCALE).then_inc(s_const, 1)
            pool.memset(tile_e[:], 0).then_inc(s_const, 1)
            pool.iota(rank_w[:], pattern=[[-1, E]], base=E, channel_multiplier=0,
                      allow_small_or_imprecise_dtypes=True).then_inc(s_const, 1)
            pool.iota(slot[:], pattern=[[1, NS], [0, E]], base=0, channel_multiplier=0,
                      allow_small_or_imprecise_dtypes=True).then_inc(s_const, 1)
            n = 11
            pool.wait_ge(s_const, n)
            row = [[1, P]]
            pool.affine_select(out=ident[:], in_=onesf[:], compare_op=ALU.is_equal, fill=0.0, base=0,
                               pattern=row, channel_multiplier=-1).then_inc(s_const, 1)
            pool.affine_select(out=ident16[:], in_=onesf[:], compare_op=ALU.is_equal, fill=0.0, base=0,
                               pattern=row, channel_multiplier=-1).then_inc(s_const, 1)
            pool.affine_select(out=upper[:], in_=onesf[:], compare_op=ALU.is_gt, fill=0.0, base=0,
                               pattern=row, channel_multiplier=-1).then_inc(s_const, 1)
            pool.affine_select(out=ones16[:], in_=onesf[:], compare_op=ALU.is_ge, fill=0.0, base=0,
                               pattern=row, channel_multiplier=0).then_inc(s_const, 1)
            pool.affine_select(out=mask_qk[:], in_=CT[:], compare_op=ALU.is_ge, fill=MASK, base=0,
                               pattern=[[-1, P]], channel_multiplier=1).then_inc(s_const, 1)
            pool.affine_select(out=mask_kq[:], in_=CT[:], compare_op=ALU.is_ge, fill=MASK, base=0,
                               pattern=row, channel_multiplier=-1).then_inc(s_const, 1)
            pool.affine_select(out=last_row[:], in_=onesf[0:1, :], compare_op=ALU.is_ge, fill=0.0, base=-LAST,
                               pattern=row, channel_multiplier=0).then_inc(s_const, 1)
            n += 7
            pool.wait_ge(s_const, n)
            pool.affine_select(out=CT[:], in_=ident[:], compare_op=ALU.is_gt, fill=-1.0, base=LAST,
                               pattern=[[0, P]], channel_multiplier=-1).then_inc(s_const, 1)
            n += 1
            pool.wait_ge(s_const, n)
            pool.affine_select(out=CT[:], in_=CT[:], compare_op=ALU.is_gt, fill=0.0, base=LAST,
                               pattern=[[-1, P]], channel_multiplier=0).then_inc(s_const, 1)
            def tick(t):
                if is_in(t):
                    pool.wait_ge(s_xa, of(t) + 1)
                    u = par(t)
                    if is_in(t - 2):
                        wait(pool, s_x2lo, of(t) - 1)
                    r2 = rs[:, 1, bass.ds(of(t) * GT, GT)].unsqueeze(2).broadcast_to([P, GT, P])
                    pool.tensor_tensor(out=x2_f[:, u, :, :],
                                       in0=xn[:, bass.ds(of(t) * GT, GT), :], in1=r2, op=ALU.mult).then_inc(s_x2f, 1)
                    pool.tensor_tensor(out=tile(x_g, of(t), GW), in0=tile(x_g, of(t), GW), in1=tile(xn_g, of(t), GW),
                                       op=ALU.add).then_inc(s_basep, 1)
                if is_in(t - 1):
                    g = of(t - 1)
                    pool.wait_ge(s_x2hi, g + 1)
                    to = x2[:, bass.ds(g * GT, GT), :]
                    pool.tensor_tensor(out=to[:, :, P:2 * P - 1], in0=x2_f[:, 1 - par(t), :, 0:LAST],
                                       in1=to[:, :, 0:LAST], op=ALU.subtract).then_inc(s_x2lo, 1)

            ticks(pool, tick)
            pool.wait_ge(s_x2lo, NG)
            pool.wait_ge(s_zeroed, 16)
            pool.wait_ge(s_pos, 1)
            for i in range(NT):
                pool.indirect_dma_start(out=sorted_x[:, :], out_offset=bass.IndirectOffsetOnAxis(
                    ap=pos[:, i:i + 1], axis=0), in_=x2[:, i, :], in_offset=None).then_inc(s_scat, 16)
            for u in range(2):
                pool.wait_ge(s_yst[u], 16 * NS // 2)
            for i in range(NT):
                pool.indirect_dma_start(out=yg[:, i, :], out_offset=None, in_=sorted_y[:, :],
                                        in_offset=bass.IndirectOffsetOnAxis(
                                            ap=pos[:, i:i + 1], axis=0)).then_inc(s_gath, 16)
            pool.wait_ge(s_gath, 16 * NT)
            yg_g = yg[:].rearrange("p (g t) d -> p g (t d)", t=GT)
            with pool.Fori(0, NG - 1) as g:
                y = yg[:, bass.ds(g * GT, GT), :]
                pool.tensor_tensor(out=y, in0=y, in1=alpha[:, bass.ds(g * GT, GT)].unsqueeze(2).broadcast_to([P, GT, P]),
                                   op=ALU.mult).then_inc(s_yal, 1)
                pool.wait_ge(s_yal, g + 1)
                pool.wait_ge(s_att, g * 2 + 2)
                pool.tensor_tensor(out=tile(x_g, g, GW), in0=tile(x_g, g, GW), in1=tile(yg_g, g, GW),
                                   op=ALU.add).then_inc(s_sum, 1)

        N_CONST = 20
        H = NT // 2

        @block.vector
        def _(v):
            chain = [0]

            def link(ins):
                chain[0] += 1
                ins.then_inc(s_dve, 1)
                v.wait_ge(s_dve, chain[0])

            def statistics(h):
                v.wait_ge(s_xin[h], 16 * NG // 2)
                for t in range(h * H, (h + 1) * H):
                    v.bn_stats(stats[:, t, :], x_sb[:, t, :]).then_inc(s_bn, 1)
                v.wait_ge(s_bn, (h + 1) * H)
                for t in range(h * H, (h + 1) * H):
                    v.bn_aggr(mv[:, t, :], stats[:, t, :]).then_inc(s_ag, 1)
                v.wait_ge(s_ag, (h + 1) * H)

            def variances(h):
                a = slice(h * H, (h + 1) * H)
                var = mv[:, a, 1:2].rearrange("p a b -> p (a b)")
                link(v.tensor_scalar(vs[:, 0, 0, a], var, EPS, None, ALU.add))
                link(v.reciprocal(nw[:, 0, 0, a], vs[:, 0, 0, a]))
                link(v.tensor_tensor(nw[:, 0, 1, a], nw[:, 0, 0, a], var, ALU.mult))
                v.tensor_scalar(vs[:, 0, 1, a], nw[:, 0, 1, a], EPS, None, ALU.add).then_inc(s_dve_roots, 1)

            def inverse_roots(h):
                a = slice(h * H, (h + 1) * H)
                v.wait_ge(s_actc, h + 1)
                v.wait_ge(s_dve_roots, h + 1)
                link(v.reciprocal(rs[:, :, a], vs[:, 1, :, a]))
                link(v.tensor_tensor(nw[:, 0, :, a], rs[:, :, a], rs[:, :, a], ALU.mult))
                link(v.tensor_tensor(nw[:, 1, :, a], nw[:, 0, :, a], vs[:, 0, :, a], ALU.mult))
                link(v.tensor_scalar(nw[:, 0, :, a], nw[:, 1, :, a], -0.5, 1.5, ALU.mult, ALU.add))
                link(v.tensor_tensor(rs[:, :, a], rs[:, :, a], nw[:, 0, :, a], ALU.mult))

            statistics(0)
            variances(0)
            statistics(1)
            variances(1)
            inverse_roots(0)
            inverse_roots(1)
            v.wait_ge(s_const, N_CONST)
            v.wait_ge(s_small, 1)
            v.tensor_copy(smallT[:], bank[0][:, 0:24]).then_inc(s_smallc, 1)
            v.tensor_copy(U_sb[:], bank[1][:, 0:P]).then_inc(s_smallc, 1)
            v.tensor_copy(ovC[:, 0:P], bank[2][:, 0:P]).then_inc(s_smallc, 1)
            v.tensor_copy(ovC[:, P:P + 1], ident[:, LAST:P]).then_inc(s_smallc, 1)

            def folded():
                v.wait_ge(s_small, 2)
                v.tensor_scalar(G_hi[:], bank[3][:, 0:P], QK_SCALE, None, ALU.mult).then_inc(s_halves, 1)
                v.tensor_scalar(cent_hi[:], bank[4][:, 0:E], QK_SCALE, None, ALU.mult).then_inc(s_halves, 1)
                v.wait_ge(s_halves, 2)
                v.scalar_tensor_tensor(out=G_lo[:], in0=bank[3][:, 0:P], scalar=QK_SCALE, in1=G_hi[:],
                                       op0=ALU.mult, op1=ALU.subtract).then_inc(s_smallc, 1)
                v.scalar_tensor_tensor(out=cent_lo[:], in0=bank[4][:, 0:E], scalar=QK_SCALE, in1=cent_hi[:],
                                       op0=ALU.mult, op1=ALU.subtract).then_inc(s_smallc, 1)

            def tick(t):
                if is_in(t):
                    g, grp = of(t), [P, GT, P]
                    on = bass.ds(g * GT, GT)
                    to = xn[:, on, :]
                    v.tensor_tensor(to, x_sb[:, on, :], mv[:, on, 0:1].broadcast_to(grp), ALU.subtract).then_inc(s_centred, 1)
                    v.wait_ge(s_centred, g + 1)
                    v.tensor_tensor(to, to, rs[:, 0, on].unsqueeze(2).broadcast_to(grp), ALU.mult).then_inc(s_xa, 1)
                if is_in(t - 1):
                    g = of(t - 1)
                    v.wait_ge(s_xahi, g + 1)
                    v.tensor_tensor(most(xa_lo, g), most(xn, g), most(xa_hi, g), ALU.subtract).then_inc(s_xalo, 1)
                    v.wait_ge(s_w2hi, g + 1)
                    v.scalar_tensor_tensor(out=tile(w2_hl, g)[:, F:2 * F], in0=w2_raw[:, par(t - 1), :], scalar=W_SCALE,
                                           in1=tile(w2_hl, g)[:, 0:F], op0=ALU.mult, op1=ALU.subtract).then_inc(s_w2lo, 1)
                if is_in(t - 2):
                    g = of(t - 2)
                    v.wait_ge(s_w1hi, g + 1)
                    v.scalar_tensor_tensor(out=tile(w1_hl, g)[:, F:2 * F], in0=bank[5 + par(t)][:], scalar=W_SCALE,
                                           in1=tile(w1_hl, g)[:, 0:F], op0=ALU.mult, op1=ALU.subtract).then_inc(s_w1lo, 1)
                if is_in(t):
                    g = of(t)
                    A = A_e[:, par(t), :]
                    v.tensor_scalar(A, CT[:], smallT[:, bass.ds(g + E, 1)], None, ALU.mult).then_inc(s_Aw, 1)
                    v.wait_ge(s_Aw, g + 1)
                    v.tensor_copy(A[:, LAST:P], smallT[:, bass.ds(g + 2 * E, 1)]).then_inc(s_Ae, 1)
                if is_in(t - 4):
                    g = of(t - 4)
                    v.wait_ge(s_qhi, g + 1)
                    v.scalar_tensor_tensor(out=cols(qT_lo, g), in0=bank[2 + par(t)][:], scalar=1.0 / QK_SCALE,
                                           in1=cols(qT_hi, g), op0=ALU.mult, op1=ALU.subtract).then_inc(s_qlo, 1)
                if isinstance(t.reg, int) and t.n == 0:
                    folded()

            ticks(v, tick)
            v.wait_ge(s_b2hi, 1)
            link(v.scalar_tensor_tensor(out=b2_lo[:], in0=b2_sb[:], scalar=W_SCALE, in1=b2_hi[:],
                                        op0=ALU.mult, op1=ALU.subtract))
            link(v.tensor_copy(b2_hl[:], b2_lo[:]))
            v.tensor_copy(b2_hl[0:1, :], b2_hi[0:1, :]).then_inc(s_b2, 1)

            v.wait_ge(s_affp, NG)
            link(v.tensor_copy(flat(aff[:]), bank[7][:, 0:NT * E]))
            v.tensor_reduce(amax[:], aff[:], AX.X, ALU.max).then_inc(s_amax, 1)
            v.wait_ge(s_amax, 1)
            wide = [P, NT, E]
            link(v.tensor_tensor(hit[:], aff[:], amax[:, :].unsqueeze(2).broadcast_to(wide), ALU.is_equal))
            link(v.tensor_tensor(hit[:], hit[:], rank_w[:, :].unsqueeze(1).broadcast_to(wide), ALU.mult))
            link(v.tensor_reduce(posf[:], hit[:], AX.X, ALU.max))
            link(v.tensor_tensor(onehot[:], hit[:], posf[:, :].unsqueeze(2).broadcast_to(wide), ALU.is_equal))
            v.tensor_copy(onehot16[:], onehot[:]).then_inc(s_onehot, 1)
            v.wait_ge(s_cnt, 1)
            link(v.tensor_copy(flat(cum[:, 0, :, :]), bank[6][:, 0:NT * E]))
            link(v.tensor_copy(below[:], bank[5][:, 0:NT * E].rearrange("p (t e) -> p t e", e=E)))
            src, step = 0, 1
            while step < NT:
                v.tensor_copy(cum[:, 1 - src, 0:step, :], cum[:, src, 0:step, :])
                link(v.tensor_tensor(cum[:, 1 - src, step:, :], cum[:, src, step:, :], cum[:, src, 0:NT - step, :], ALU.add))
                src, step = 1 - src, 2 * step
            link(v.tensor_scalar(cnt_i[:], cum[:, src, NT - 1, :], float(FW - 1), None, ALU.add))
            link(v.tensor_tensor(below[:, 1:, :], below[:, 1:, :], cum[:, src, 0:NT - 1, :], ALU.add))
            link(v.tensor_scalar(tiles_i[:], cnt_i[:], FW.bit_length() - 1, None, ALU.arith_shift_right))
            link(v.tensor_copy(tcum[:, 0, :], tiles_i[:]))
            link(v.tensor_copy(tiles_f[:], tiles_i[:]))
            src, step = 0, 1
            while step < E:
                v.tensor_copy(tcum[:, 1 - src, 0:step], tcum[:, src, 0:step])
                link(v.tensor_tensor(tcum[:, 1 - src, step:], tcum[:, src, step:], tcum[:, src, 0:E - step], ALU.add))
                src, step = 1 - src, 2 * step
            link(v.tensor_tensor(base[:], tcum[:, src, :], tiles_f[:], ALU.subtract))
            link(v.tensor_tensor(slot_hit[:], slot[:], base[0:1, :].unsqueeze(1).broadcast_to([1, NS, E]), ALU.is_ge))
            link(v.tensor_reduce(tile_ef[:], slot_hit[:], AX.X, ALU.add))
            v.tensor_scalar(tile_e[:, 0:NS], tile_ef[:], -1.0, None, ALU.add).then_inc(s_tile_e, 1)
            link(v.tensor_scalar(base[:], base[:], float(FW), None, ALU.mult))
            link(v.tensor_tensor(below[:], below[:], base[:, :].unsqueeze(1).broadcast_to(wide), ALU.add))
            link(v.tensor_tensor(below[:], below[:], onehot[:], ALU.mult))
            link(v.tensor_reduce(posf[:], below[:], AX.X, ALU.add))
            link(v.tensor_copy(pos[:], posf[:]))
            v.sem_inc(s_pos, 1)
            v.wait_ge(s_actc, 3)
            link(v.tensor_scalar(eneg[:], eneg[:], 1.0, None, ALU.add))
            link(v.reciprocal(alpha[:], eneg[:]))

            def reduce_unit(n, par, i, c, width, wait_extra=None):
                v.wait_ge(s_max_mm, n + 1)
                v.tensor_reduce(row_max[:, i, c:c + 1] if isinstance(c, int) else row_max[:, i, bass.ds(c, 1)],
                                bank[2 + par][:, 0:width], AX.X, ALU.max).then_inc(s_max, 1)

            def shift(b, g, units_done, nth):
                v.wait_ge(s_max, units_done)
                if g:
                    link(v.tensor_reduce(row_m[:], row_max[:, :, 0:g + 1], AX.X, ALU.max))
                    m = row_m[:]
                else:
                    m = row_max[:, :, 0]
                v.tensor_scalar(neg_max[:, :, LAST], m, -1.0, SHIFT, ALU.mult, ALU.add).then_inc(s_neg, 1)
                v.wait_ge(s_negT, nth + 1)
                q = qT_hi[96:P, (b * BG + g) * GW:(b * BG + g + 1) * GW]
                v.tensor_tensor(q, q, bank[5][96:P, :], ALU.add).then_inc(s_shift, 1)

            def weights_low(n, par, off):
                v.wait_ge(s_exp, n + 1)
                wait(v, s_pvlo, n - 1)
                v.tensor_tensor(p_lo[:, par, off:GW], p_sb[:, par, off:GW], p_hi[:, par, off:GW],
                                ALU.subtract).then_inc(s_plo, 1)

            def attention(b):
                n0 = b * STEPS
                for i in range(GT):
                    reduce_unit(n0 + i, i % 2, i, 0, (i + 1) * P)
                shift(b, 0, n0 + GT, b * BG)
                u0 = n0 + GT
                for g in range(BG):
                    more = g + 1 < BG
                    if g:
                        with v.Fori(0, g) as c:
                            for i in range(GT):
                                if more:
                                    reduce_unit(c * GT + (u0 + i), i % 2, i, c, GW)
                                weights_low(c * GT + (n0 + i), i % 2, 0)
                    for i in range(GT):
                        if more:
                            reduce_unit(u0 + g * GT + i, i % 2, i, g, GW)
                        weights_low(n0 + g * GT + i, i % 2, i * P)
                    if more:
                        for i in range(GT):
                            reduce_unit(u0 + (g + 1) * GT + i, i % 2, i, g + 1, (i + 1) * P)
                        u0 += GT * (g + 2)
                        shift(b, g + 1, u0, b * BG + g + 1)
                    n0 += GT * (g + 1)
                    for f in range(2):
                        n = (b * BG + g) * 2 + f
                        v.wait_ge(s_fin, n + 1)
                        o = bank[6 + f][:, 0:2 * (P + 1)].rearrange("p (t d) -> p t d", t=2)
                        wait(v, s_att, n - 1)
                        link(v.reciprocal(inv_den[:, f, :], o[:, :, P]))
                        for t in range(2):
                            dst = x_sb[:, (b * BG + g) * GT + f * 2 + t, :]
                            ins = v.scalar_tensor_tensor(out=dst, in0=o[:, t, 0:P], scalar=inv_den[:, f, t:t + 1], in1=dst,
                                                         op0=ALU.mult, op1=ALU.add)
                        ins.then_inc(s_att, 1)

            def ffn():
                def lows(k, u):
                    v.wait_ge(s_hhi, k + 1)
                    v.scalar_tensor_tensor(out=h_lo[:, u, :], in0=hidden_ps[u], scalar=0.0, in1=h_hi[:, u, :],
                                           op0=ALU.max, op1=ALU.subtract).then_inc(s_hlo, 1)

                def turned(k, u):
                    v.wait_ge(s_tr, k + 1)
                    v.tensor_copy(x2T[:, u, :], bank[6 + u][:].bitcast(F16)[:, 0:2 * FW]).then_inc(s_x2T, 1)

                turned(0, 0)
                turned(1, 1)
                lows(0, 0)
                turned(2, 0)
                lows(1, 1)
                turned(3, 1)
                with v.Fori(1, NS // 2 - 1) as r:
                    for u in range(2):
                        lows(r * 2 + u, u)
                        turned(r * 2 + (u + 2), u)
                for u in range(2):
                    lows(NS - 2 + u, u)

            def last_group():
                v.wait_ge(s_gath, 16 * NT)
                v.wait_ge(s_att, 2 * NG)
                for i in range((NG - 1) * GT, NT):
                    ins = v.scalar_tensor_tensor(out=x_sb[:, i, :], in0=yg[:, i, :], scalar=alpha[:, i:i + 1],
                                                 in1=x_sb[:, i, :], op0=ALU.mult, op1=ALU.add)
                ins.then_inc(s_sum_last, 1)

            v.wait_ge(s_basep, NG)
            attention(0)
            ffn()
            attention(1)
            last_group()

        @block.scalar
        def _(a):
            for dst, src in ((small[0:8, :], cent), (small[8:16, :], ln_g), (small[16:24, :], ln_b),
                             (qk_sb[:], qk), (ov_sb[:], ov),
                             (b2_sb[0:1, :], b2.rearrange("(o e) f -> o (e f)", o=1)),
                             (b2_sb[1:2, :], b2.rearrange("(o e) f -> o (e f)", o=1))):
                a.dma_start(dst, src).then_inc(s_win, 16)
            for h in range(2):
                t = slice(h * H, (h + 1) * H)
                a.wait_ge(s_dve_roots, h + 1)
                a.activation(vs[:, 1, :, t], vs[:, 0, :, t], ACT.Sqrt).then_inc(s_actc, 1)

            def tick(t):
                if is_in(t):
                    g = of(t)
                    a.wait_ge(s_xa, g + 1)
                    a.activation(most(xa_hi, g), most(xn, g), ACT.Copy).then_inc(s_xahi, 1)
                    u = par(t)
                    a.wait_ge(s_wl[1][u], (g - u) * 8 + 16)
                    a.activation(tile(w2_hl, g)[:, 0:F], w2_raw[:, u, :], ACT.Copy, scale=W_SCALE).then_inc(s_w2hi, 1)
                if is_in(t - 2):
                    g = of(t - 2)
                    a.wait_ge(s_kp, g + 1)
                    for half, to, s in ((0, kT_hi, s_khi), (1, kT_lo, s_klo)):
                        a.activation(cols(to, g), bank[par(t)][:].bitcast(F16)[:, half * GW:(half + 1) * GW],
                                     ACT.Copy).then_inc(s, 1)
                if is_in(t - 1):
                    g = of(t - 1)
                    a.wait_ge(s_w1p, g + 1)
                    a.activation(tile(w1_hl, g)[:, 0:F], bank[5 + par(t - 1)][:], ACT.Copy, scale=W_SCALE).then_inc(s_w1hi, 1)
                    a.wait_ge(s_x2f, g + 1)
                    a.activation(x2[:, bass.ds(g * GT, GT), 0:LAST], x2_f[:, par(t - 1), :, 0:LAST], ACT.Copy).then_inc(s_x2hi, 1)
                if is_in(t - 3):
                    g = of(t - 3)
                    a.wait_ge(s_qp, g + 1)
                    a.activation(cols(qT_hi, g), bank[2 + par(t - 3)][:], ACT.Copy, scale=1.0 / QK_SCALE).then_inc(s_qhi, 1)

            ticks(a, tick)
            a.wait_ge(s_win, 16 * 7)
            a.activation(b2_hi[:], b2_sb[:], ACT.Copy, scale=W_SCALE).then_inc(s_b2hi, 1)
            a.wait_ge(s_amax, 1)
            a.activation(eneg[:], amax[:], ACT.Exp, scale=-1.0 / QK_SCALE).then_inc(s_actc, 1)

            def exp_step(n, par, off):
                a.wait_ge(s_sc, n + 1)
                wait(a, s_pv, n - 1)
                wait(a, s_plo, n - 1)
                a.activation(p_hi[:, par, off:GW], bank[par][:, off:GW], ACT.Exp, scale=SCALE).then_inc(s_phi, 1)
                a.activation(p_sb[:, par, off:GW], bank[par][:, off:GW], ACT.Exp, scale=SCALE).then_inc(s_exp, 1)

            def attention(b):
                n0 = b * STEPS
                for g in range(BG):
                    if g:
                        with a.Fori(0, g) as c:
                            for i in range(GT):
                                exp_step(c * GT + (n0 + i), i % 2, 0)
                    for i in range(GT):
                        exp_step(n0 + g * GT + i, i % 2, i * P)
                    n0 += GT * (g + 1)
                    a.wait_ge(s_pvlo, n0)
                    if b * BG + g:
                        a.wait_ge(s_fin, 2 * (b * BG + g))
                    a.activation(oT[:], bank[4][:], ACT.Copy).then_inc(s_oT, 1)

            def ffn():
                def highs(k, u):
                    a.wait_ge(s_z, k + 1)
                    a.activation(h_hi[:, u, :], hidden_ps[u], ACT.Relu).then_inc(s_hhi, 1)

                def rows(k, u):
                    a.wait_ge(s_y, k + 1)
                    if not isinstance(k, int) or k >= 2:
                        a.wait_ge(s_yst[u], (k - u) * 8)
                    a.activation(y_sb[:, u, :], bank[4 + u][:, 0:FT * P], ACT.Copy,
                                 scale=1.0 / (W_SCALE * W_SCALE)).then_inc(s_ysb, 1)

                highs(0, 0)
                for k in range(2):
                    highs(k + 1, (k + 1) % 2)
                    rows(k, k % 2)
                with a.Fori(1, NS // 2 - 1) as r:
                    for u in range(2):
                        highs(r * 2 + (u + 1), 1 - u)
                        rows(r * 2 + u, u)
                highs(NS - 1, 1)
                rows(NS - 2, 0)
                rows(NS - 1, 1)

            attention(0)
            ffn()
            attention(1)

        @block.tensor
        def _(pe):
            pe.wait_ge(s_const, N_CONST)
            pe.wait_ge(s_win, 16 * 7)
            mm = pe.matmul
            pe.transpose(bank[0][:, 0:24], small[:], ident[0:24, 0:24])
            mm(bank[1][:, 0:P], qk_sb[:], CT[:], start=True, stop=True)
            mm(bank[2][:, 0:P], CT[:], ov_sb[:], start=True, stop=True).then_inc(s_small, 1)
            pe.wait_ge(s_smallc, 4)
            mm(bank[4][:, 0:E], CT[:], smallT[:, 0:E], start=True, stop=True)
            mm(bank[3][:, 0:P], U_sb[:], CT[:], start=True, stop=True).then_inc(s_small, 1)
            pe.wait_ge(s_smallc, 6)

            def tick(t):
                if is_in(t - 3):
                    g = of(t - 3)
                    pe.wait_ge(s_klo, g + 1)
                    if is_in(t - 5):
                        pe.wait_ge(s_qlo, g - 1)
                    q = bank[2 + par(t - 3)][:]
                    mm(q, G_hi[:], cols(kT_hi, g), start=True, stop=False)
                    mm(q, G_hi[:], cols(kT_lo, g), start=False, stop=False)
                    mm(q, G_lo[:], cols(kT_hi, g), start=False, stop=True).then_inc(s_qp, 1)
                    for i in range(GT):
                        hi, lo = (k[:, bass.ds(g * GW + i * P, P)] for k in (kT_hi, kT_lo))
                        to = bank[7][:, bass.ds(g * (GT * E) + i * E, E)]
                        mm(to, hi, cent_hi[:], start=True, stop=False)
                        mm(to, hi, cent_lo[:], start=False, stop=False)
                        m = mm(to, lo, cent_hi[:], start=False, stop=True)
                    m.then_inc(s_affp, 1)
                if is_in(t - 2):
                    g = of(t - 2)
                    pe.wait_ge(s_xalo, g + 1)
                    for half, x16 in enumerate((xa_hi, xa_lo)):
                        for i in range(GT):
                            c = half * GW + i * P
                            m = pe.transpose(bank[par(t)][:].bitcast(F16)[:, c:c + P], tile(x16, g * GT + i), ident16[:])
                    m.then_inc(s_kp, 1)
                if is_in(t):
                    g, u = of(t), par(t)
                    pe.wait_ge(s_Ae, g + 1)
                    pe.wait_ge(s_wl[0][u], (g - u) * 8 + 16)
                    pe.wait_ge(s_wl[2][u], (g - u) * 8 + 16)
                    if is_in(t - 2):
                        pe.wait_ge(s_w1lo, g - 1)
                    mm(bank[5 + u][:], A_e[:, u, :], w1_raw[:, u, :], start=True, stop=False)
                    mm(bank[5 + u][:], last_row[:], b1_raw[:, u, :], start=False, stop=True).then_inc(s_w1p, 1)

            ticks(pe, tick)
            pe.wait_ge(s_w1lo, E)
            pe.wait_ge(s_onehot, 1)
            oh = onehot16[:].rearrange("p t e -> p (t e)")
            mm(bank[5][:, 0:NT * E], upper[:], oh, start=True, stop=True)
            mm(bank[6][:, 0:NT * E], ones16[:], oh, start=True, stop=True).then_inc(s_cnt, 1)

            def max_unit(n, b, g, par, i, c, width):
                wait(pe, s_max, n - 1)
                q = (b * BG + g) * GW + i * P
                diag = width is not None
                w = width or GW
                dst = bank[2 + par][:, 0:w]
                first = mm(dst, qT_hi[:, q:q + P], kT_hi[:, bass.ds(c * GW + b * S, w)], start=True, stop=not diag)
                if diag:
                    mm(bank[2 + par][:, w - P:w], ident16[:], mask_qk[:], start=False, stop=True).then_inc(s_max_mm, 1)
                else:
                    pe_last[0].then_inc(s_max_mm, 1)

            pe_last = [None]

            def mmk(*args, **kw):
                pe_last[0] = pe.matmul(*args, **kw)
                return pe_last[0]

            mm = mmk

            def shift(b, g):
                nth = b * BG + g
                pe.wait_ge(s_neg, nth + 1)
                for i in range(GT):
                    t = mm(bank[5][:, i * P:(i + 1) * P], neg_max[:, i, :], ident16[:], start=True, stop=True)
                t.then_inc(s_negT, 1)

            def scores(n, b, g, par, j, off):
                wait(pe, s_exp, n - 1)
                q = slice((b * BG + g) * GW + off, (b * BG + g + 1) * GW)
                k = bass.ds(j * P + b * S, P) if not isinstance(j, int) else slice(b * S + j * P, b * S + (j + 1) * P)
                dst = bank[par][:, off:GW]
                mm(dst, kT_hi[:, k], qT_hi[:, q], start=True, stop=False)
                mm(dst, kT_hi[:, k], qT_lo[:, q], start=False, stop=False)
                diag = isinstance(j, int) and j >= g * GT
                mm(dst, kT_lo[:, k], qT_hi[:, q], start=False, stop=not diag)
                if diag:
                    mm(bank[par][:, off:off + P], ident16[:], mask_kq[:], start=False, stop=True)
                pe_last[0].then_inc(s_sc, 1)

            def rows(t, b, j):
                return tile(t, j + b * BT)

            def weighted(n, b, g, par, j, off):
                first = isinstance(j, int) and j == 0
                if first:
                    wait(pe, s_oT, b * BG + g)
                pe.wait_ge(s_phi, n + 1)
                to, w = bank[4][:, off:GW], p_hi[:, par, off:GW]
                mm(to, rows(xa_hi, b, j), w, start=first, stop=False, skip_group_check=True)
                mm(to, rows(xa_lo, b, j), w, start=False, stop=False, skip_group_check=True).then_inc(s_pv, 1)

            def weighted_low(n, b, g, par, j, off):
                pe.wait_ge(s_plo, n + 1)
                last = isinstance(j, int) and j == g * GT + GT - 1
                mm(bank[4][:, off:GW], rows(xa_hi, b, j), p_lo[:, par, off:GW], start=False, stop=last,
                   skip_group_check=True).then_inc(s_pvlo, 1)

            def project(b, g):
                nth = b * BG + g
                pe.wait_ge(s_oT, nth + 1)
                if nth:
                    pe.wait_ge(s_att, 2 * nth)
                for f in range(2):
                    for t in range(2):
                        i = f * 2 + t
                        m = mm(bank[6 + f][:, t * (P + 1):(t + 1) * (P + 1)], oT[:, i * P:(i + 1) * P], ovC[:],
                               start=True, stop=True)
                    m.then_inc(s_fin, 1)

            def attention(b):
                n0 = b * STEPS
                for i in range(GT):
                    max_unit(n0 + i, b, 0, i % 2, i, 0, (i + 1) * P)
                shift(b, 0)
                u0 = n0 + GT
                for g in range(BG):
                    more = g + 1 < BG
                    diag = g * GT

                    def step(c, i, first=False):
                        j = c * GT + i
                        on = isinstance(c, int) and c == g
                        if not (on and i == GT - 1):
                            scores(j + (n0 + 1), b, g, (i + 1) % 2, j + 1, (i + 1) * P if on else 0)
                        if more:
                            max_unit(j + u0, b, g + 1, i % 2, i, c, None)
                        if not first:
                            weighted_low(j + (n0 - 1), b, g, (i + 1) % 2, j - 1, (i - 1) * P if on and i else 0)
                        weighted(j + n0, b, g, i % 2, j, i * P if on else 0)

                    pe.wait_ge(s_shift, b * BG + g + 1)
                    scores(n0, b, g, 0, 0, 0)
                    for i in range(GT - 1 if g else GT):
                        step(0, i, first=(i == 0))
                    if g > 1:
                        with pe.Fori(1, g) as c:
                            step(c - 1, GT - 1)
                            for i in range(GT - 1):
                                step(c, i)
                    if g:
                        step(g - 1, GT - 1)
                        for i in range(GT):
                            step(g, i)
                    weighted_low(n0 + diag + GT - 1, b, g, 1, diag + GT - 1, (GT - 1) * P)
                    if more:
                        for i in range(GT):
                            max_unit(u0 + diag + GT + i, b, g + 1, i % 2, i, g + 1, (i + 1) * P)
                        shift(b, g + 1)
                        u0 += GT * (g + 2)
                    n0 += GT * (g + 1)
                    project(b, g)

            def ffn():
                pe.wait_ge(s_tile_e, 1)
                pe.wait_ge(s_b2, 1)

                def turn(k, u):
                    wait(pe, s_x2T, k - 1)
                    pe.wait_ge(s_xs[u], (k - u) * 8 + 16)
                    for half in range(2):
                        for t in range(FT):
                            m = pe.transpose(bank[6 + u][:].bitcast(F16)[:, half * FW + t * P:half * FW + (t + 1) * P],
                                             xs_sb[:, u, t, half * P:(half + 1) * P], ident16[:])
                    m.then_inc(s_tr, 1)

                def hidden(k, u, e):
                    pe.wait_ge(s_x2T, k + 1)
                    wait(pe, s_hlo, k - 1)
                    for c in range(FC):
                        dst = hidden_ps[u][:, c * FW:(c + 1) * FW]
                        hi = w1_flat[:, bass.ds(e * (2 * F) + c * P, P)]
                        lo = w1_flat[:, bass.ds(e * (2 * F) + (F + c * P), P)]
                        mm(dst, hi, x2T[:, u, 0:FW], start=True, stop=False)
                        mm(dst, hi, x2T[:, u, FW:2 * FW], start=False, stop=False)
                        m = mm(dst, lo, x2T[:, u, 0:FW], start=False, stop=True)
                    m.then_inc(s_z, 1)

                def output(k, u, e):
                    wait(pe, s_ysb, k - 1)
                    pe.wait_ge(s_hlo, k + 1)
                    to = [bank[4 + u][:, t * P:(t + 1) * P] for t in range(FT)]
                    for t in range(FT):
                        mm(to[t], row16[:], b2_hl[:, bass.ds(e * P, P)], start=(t == 0), stop=False, skip_group_check=True)
                    for c in range(FC):
                        hi = w2_flat[:, bass.ds(e * (2 * F) + c * P, P)]
                        lo = w2_flat[:, bass.ds(e * (2 * F) + (F + c * P), P)]
                        for t in range(FT):
                            at = slice(c * FW + t * P, c * FW + (t + 1) * P)
                            mm(to[t], h_hi[:, u, at], hi, start=False, stop=False, skip_group_check=True)
                            mm(to[t], h_hi[:, u, at], lo, start=False, stop=False, skip_group_check=True)
                            m = mm(to[t], h_lo[:, u, at], hi, start=False, stop=(c == FC - 1), skip_group_check=True)
                    m.then_inc(s_y, 1)

                def experts(k, n=4):
                    _, values = nc.values_load_multi_w_load_instructions(
                        tile_e[0:1, bass.ds(k, n)], engines=[mybir.EngineType.PE], min_val=0, max_val=E - 1,
                        skip_runtime_bounds_check_because="a count of at most E experts, less one")
                    return values

                def round2(k, last=False):
                    e = experts(k)
                    for u in range(2):
                        output(k + u, u, e[u])
                        if not (isinstance(k, int) and k + u + 2 >= NS):
                            hidden(k + u + 2, u, e[u + 2])
                        if not (isinstance(k, int) and k + u + 3 >= NS):
                            turn(k + u + 3, 1 - u)

                turn(0, 0)
                turn(1, 1)
                e = experts(0)
                hidden(0, 0, e[0])
                turn(2, 0)
                hidden(1, 1, e[1])
                round2(0)
                with pe.Fori(1, NS // 2 - 2) as r:
                    round2(r * 2)
                round2(NS - 4)
                round2(NS - 2)

            attention(0)
            pe.wait_ge(s_exp, STEPS)
            pe.wait_ge(s_max, STEPS)
            pe.wait_ge(s_att, 2 * BG)
            ffn()
            pe.wait_ge(s_hlo, NS)
            pe.wait_ge(s_ysb, NS)
            attention(1)


_INS = ['L0_attn_input_data', 'L0_attn_qk', 'L0_attn_ov', 'L0_ffn_centroids', 'L0_ffn_ln_g', 'L0_ffn_ln_b',
        'L0_ffn_w1', 'L0_ffn_b1', 'L0_ffn_w2', 'L0_ffn_b2']


def kernel(**inputs):
    import numpy as _np
    import concourse.bacc as _bacc
    from concourse import mybir as _mybir
    from concourse.bass_utils import run_bass_kernel_spmd as _run

    nc = _bacc.Bacc("TRN2", target_bir_lowering=False, num_devices=1)
    arrays, args = {}, []
    for name in _INS:
        a = _np.ascontiguousarray(inputs[name])
        arrays[f"in_{name}"] = a
        args.append(nc.dram_tensor(f"in_{name}", a.shape, _mybir.dt.from_np(a.dtype), kind="ExternalInput").ap())
    B, S, D = inputs['L0_attn_input_data'].shape
    E = inputs['L0_ffn_w1'].shape[0]
    rows = B * S + E * 256
    args.append(nc.dram_tensor("sorted_x", (rows, 2 * D), _mybir.dt.float16, kind="Internal").ap())
    args.append(nc.dram_tensor("sorted_y", (rows, D), _mybir.dt.float32, kind="Internal").ap())
    args.append(nc.dram_tensor("out", (B, S, D), _mybir.dt.float32, kind="ExternalOutput").ap())
    build(nc, *args)
    r = _run(nc, [arrays], core_ids=[0])
    return r.results[0]["out"]
```

```python
import concourse.bass as bass
from concourse import mybir
from contextlib import ExitStack

F32 = mybir.dt.float32
F16 = mybir.dt.float16
BF16 = mybir.dt.bfloat16
I32 = mybir.dt.int32
U32 = mybir.dt.uint32
ALU = mybir.AluOpType
ACT = mybir.ActivationFunctionType
AX = mybir.AxisListType

P = 128
EPS = 1e-5
W_SCALE = 16.0
QK_SCALE = 64.0
SHIFT = 32.0
MASK = -1e30
LAST = P - 1


def flat(ap):
    return ap.rearrange("p a b -> p (a b)")


def build(nc, x, qk, ov, cent, ln_g, ln_b, w1, b1, w2, b2, sorted_x, sorted_y, out):
    B, S, D = x.shape
    E, _, F = w1.shape
    assert D == P and B == 2 and E & (E - 1) == 0
    N = B * S
    NT = N // P
    GT = 4
    GW = GT * P
    NG = N // GW
    NQ = 4
    BG = S // GW
    BT = S // P
    FC = F // P
    FT = 2
    FW = FT * P
    NS = NT // FT + E - 1
    UNITS = [GT * (g + 1) for g in range(BG)]
    STEPS = sum(UNITS)
    SCALE = float(D) ** -0.5

    x_t = x.rearrange("b (t p) d -> p (b t) d", p=P)
    out_t = out.rearrange("b (t p) d -> p (b t) d", p=P)

    with ExitStack() as ctx:
        def sb(name, shape, dt=F32):
            return ctx.enter_context(nc.sbuf_tensor(name, shape, dt))

        def sem(name):
            return ctx.enter_context(nc.semaphore(name))

        x_sb = sb("x_sb", [P, NT, P])
        xn = sb("xn", [P, NT, P])
        yg = xn
        xa_hi = sb("xa_hi", [P, NT, P], F16)
        xa_lo = sb("xa_lo", [P, NT, P], F16)
        x2 = sb("x2", [P, NT, 2 * P], F16)
        kT_hi = sb("kT_hi", [P, N], F16)
        kT_lo = sb("kT_lo", [P, N], F16)
        qT_hi = sb("qT_hi", [P, N], F16)
        qT_lo = sb("qT_lo", [P, N], F16)
        w1_raw = sb("w1_raw", [P, 2, F])
        w2_raw = sb("w2_raw", [P, 2, F])
        b1_sb = sb("b1_sb", [2 * E, F])
        b1_hi = sb("b1_hi", [2 * E, F], F16)
        b1_hl = sb("b1_hl", [2 * E, F], F16)
        pick = sb("pick", [2 * E, E, P], F16)
        pick_last = sb("pick_last", [2 * E, E, P], F16)
        x2_f = sb("x2_f", [P, 2, GT, P])
        w1_hl = sb("w1_hl", [P, E, 2 * F], F16)
        w2_hl = sb("w2_hl", [P, E, 2 * F], F16)
        b2_sb = sb("b2_sb", [2 * E, P])
        b2_hi = sb("b2_hi", [2 * E, P], F16)
        b2_hl = sb("b2_hl", [2 * E, P], F16)
        small = sb("small", [3 * 8, P])
        smallT = sb("smallT", [P, 3 * 8])
        cent_hi = sb("cent_hi", [P, E], F16)
        cent_lo = sb("cent_lo", [P, E], F16)
        qk_sb = sb("qk_sb", [P, P])
        ov_sb = sb("ov_sb", [P, P])
        ovC = sb("ovC", [P, P + 1])
        U_sb = sb("U_sb", [P, P])
        G_hi = sb("G_hi", [P, P], F16)
        G_lo = sb("G_lo", [P, P], F16)
        A_e = sb("A_e", [P, 2, P])
        ident = sb("ident", [P, P])
        ident16 = sb("ident16", [P, P], F16)
        CT = sb("CT", [P, P])
        onesf = sb("onesf", [P, P])
        ones16 = sb("ones16", [P, P], F16)
        upper = sb("upper", [P, P], F16)
        mask_qk = sb("mask_qk", [P, P], BF16)
        mask_kq = sb("mask_kq", [P, P], BF16)
        stats = sb("stats", [P, NT, 6])
        mv = sb("mv", [P, NT, 2])
        vs = sb("vs", [P, 2, 2, NT])
        rs = sb("rs", [P, 2, NT])
        nw = sb("nw", [P, 2, 2, NT])
        aff = sb("aff", [P, NT, E])
        amax = sb("amax", [P, NT])
        eneg = sb("eneg", [P, NT])
        alpha = sb("alpha", [P, NT])
        hit = sb("hit", [P, NT, E])
        rank_w = sb("rank_w", [P, E])
        onehot = sb("onehot", [P, NT, E])
        onehot16 = sb("onehot16", [P, NT, E], F16)
        cum = sb("cum", [P, 2, NT, E])
        below = sb("below", [P, NT, E])
        tiles_f = sb("tiles_f", [P, E])
        tcum = sb("tcum", [P, 2, E])
        base = sb("base", [P, E])
        base_rows = sb("base_rows", [P, E])
        posf = sb("posf", [P, NT])
        pos = sb("pos", [P, NT], U32)
        slot = sb("slot", [1, NS, E])
        slot_hit = sb("slot_hit", [1, NS, E])
        tile_ef = sb("tile_ef", [1, NS])
        tile_e = sb("tile_e", [1, NS + 4], I32)
        zero = sb("zero", [P, 2 * P], F16)
        row_max = sb("row_max", [P, GT, BG])
        row_m = sb("row_m", [P, GT])
        neg_max = sb("neg_max", [P, GT, P], F16)
        p_sb = sb("p_sb", [P, 2, GW])
        p_hi = sb("p_hi", [P, 2, GW], F16)
        p_lo = sb("p_lo", [P, 2, GW], F16)
        oT = sb("oT", [P, GW])
        inv_den = sb("inv_den", [P, 2, 2])
        xs_sb = sb("xs_sb", [P, 2, FT, 2 * P], F16)
        x2T = sb("x2T", [P, 2, 2 * FW], F16)
        h_hi = sb("h_hi", [P, 2, FC * FW], F16)
        h_lo = sb("h_lo", [P, 2, FC * FW], F16)
        y_sb = sb("y_sb", [P, 2, FT * P])

        psum = ctx.enter_context(nc.psum_tensor("psum", [P, 8, 512], F32))
        bank = [psum[:, i, :] for i in range(8)]

        s_xin = [sem(f"s_xin{i}") for i in range(NQ)]
        s_bn = sem("s_bn")
        s_ag = sem("s_ag")
        s_centred = sem("s_centred")
        s_x2f = sem("s_x2f")
        s_sum_b1 = sem("s_sum_b1")
        s_win = sem("s_win")
        s_bias = sem("s_bias")
        s_wl = [[sem(f"s_wl{i}{u}") for u in range(2)] for i in range(2)]
        s_core = sem("s_core")
        s_const = sem("s_const")
        s_w2s = sem("s_w2s")
        s_dve = sem("s_dve")
        s_actc = sem("s_actc")
        s_small = sem("s_small")
        s_smallc = sem("s_smallc")
        s_xa = sem("s_xa")
        s_basep = sem("s_basep")
        s_x2hi = sem("s_x2hi")
        s_xahi = sem("s_xahi")
        s_xalo = [sem(f"s_xalo{i}") for i in range(2)]
        s_kp = sem("s_kp")
        s_khi = sem("s_khi")
        s_klo = sem("s_klo")
        s_phi = sem("s_phi")
        s_plo = [sem(f"s_plo{i}") for i in range(2)]
        s_pvlo = sem("s_pvlo")
        s_qp = sem("s_qp")
        s_qhi = sem("s_qhi")
        s_qlo = sem("s_qlo")
        s_affp = sem("s_affp")
        s_Ae = sem("s_Ae")
        s_w1p = sem("s_w1p")
        s_w1hi = sem("s_w1hi")
        s_w1lo = sem("s_w1lo")
        s_w2hi = sem("s_w2hi")
        s_w2lo = sem("s_w2lo")
        s_cnt = sem("s_cnt")
        s_onehot = sem("s_onehot")
        s_tile_e = sem("s_tile_e")
        s_zero = sem("s_zero")
        s_zeroed = sem("s_zeroed")
        s_scat = sem("s_scat")
        s_max_mm = sem("s_max_mm")
        s_max = sem("s_max")
        s_neg = sem("s_neg")
        s_negT = sem("s_negT")
        s_shift = sem("s_shift")
        s_sc = sem("s_sc")
        s_exp = sem("s_exp")
        s_pv = sem("s_pv")
        s_oT = sem("s_oT")
        s_fin = sem("s_fin")
        s_att = sem("s_att")
        s_xs = [sem(f"s_xs{i}") for i in range(2)]
        s_tr = sem("s_tr")
        s_x2T = sem("s_x2T")
        s_z = sem("s_z")
        s_hhi = sem("s_hhi")
        s_hlo = sem("s_hlo")
        s_y = sem("s_y")
        s_ysb = sem("s_ysb")
        s_yst = [sem(f"s_yst{i}") for i in range(2)]
        s_gath = [sem(f"s_gath{b}") for b in range(B)]
        s_sum = sem("s_sum")
        s_out = sem("s_out")
        s_yal = sem("s_yal")
        s_halves = sem("s_halves")
        s_bias_hi = sem("s_bias_hi")
        s_bias_hl = sem("s_bias_hl")
        s_choose = sem("s_choose")
        s_sort = sem("s_sort")
        s_blocks = sem("s_blocks")
        s_base = sem("s_base")
        s_cntc = sem("s_cntc")
        s_dve_roots = sem("s_dve_roots")
        s_x2lo = sem("s_x2lo")
        s_Aw = sem("s_Aw")
        s_amax = sem("s_amax")

        def tile(t, i, n=P):
            return flat(t[:, bass.ds(i, 1), :])

        def most(t, g):
            return t[:, bass.ds(g * GT, GT), 0:LAST]

        xn_g, x_g = (t[:].rearrange("p (g t) d -> p g (t d)", t=GT) for t in (xn, x_sb))

        w1_flat, w2_flat = (flat(t[:]) for t in (w1_hl, w2_hl))
        hidden_ps = [psum[:, b0:b0 + 2, :].rearrange("p a b -> p (a b)") for b0 in (2, 0)]

        def cols(t, i, n=GW):
            return t[:, bass.ds(i * n, n)]

        def wait(eng, s, n):
            if not isinstance(n, int) or n > 0:
                eng.wait_ge(s, n)

        LAGS = 4

        class Tick:

            def __init__(self, reg, n):
                self.reg, self.n = reg, n

            def __add__(self, k):
                return Tick(self.reg, self.n + k)

            def __sub__(self, k):
                return Tick(self.reg, self.n - k)

        def of(t):
            return t.n if isinstance(t.reg, int) else t.reg + t.n

        def par(t):
            return t.n % 2

        def static(t):
            return isinstance(t.reg, int)

        def is_in(t):
            return not static(t) or 0 <= t.n < NG

        def first_units(t):
            return {NG: (0,), NG + 1: (1,), NG + 2: (2, 3)}.get(t.n, ()) if static(t) else ()

        def by_vector(t):
            return static(t) and t.n == NG - 1

        def ticks(eng, tick):
            for n in range(LAGS):
                tick(Tick(0, n))
            with eng.Fori(LAGS // 2, NG // 2) as r:
                for u in range(2):
                    tick(Tick(r * 2, u))
            for n in range(NG, NG + LAGS + 1):
                tick(Tick(0, n))

        MAX_PLAN = []
        for g in range(BG):
            MAX_PLAN += [(g, c, i) for c in range(g + 1) for i in range(GT)] + [(g,)]

        def max_work(m, unit, shift):
            work = []
            for k in (2 * m, 2 * m + 1):
                if k < len(MAX_PLAN):
                    what = MAX_PLAN[k]
                    n = STEPS + k - what[0]
                    if len(what) == 1:
                        work.append(lambda g=what[0]: shift(g))
                    else:
                        g, c, i = what
                        work.append(lambda n=n, g=g, c=c, i=i: unit(n, g, c, i, (i + 1) * P if c == g else None))
                else:
                    work.append(lambda: None)
            return work

        LOW_POOL = 4

        def sum_bank(b, g):
            return bank[5 - g % 2 if b else 4]

        def lows_done(n):
            if isinstance(n, int) and n < LOW_POOL:
                return s_plo[0], n + 1
            return s_plo[1], n + 1 - LOW_POOL

        def weights_low(eng, n, par, off):
            eng.wait_ge(s_exp, n + 1)
            wait(eng, s_pvlo, n - 1)
            done, _ = lows_done(n)
            eng.tensor_tensor(out=p_lo[:, par, off:GW], in0=p_sb[:, par, off:GW], in1=p_hi[:, par, off:GW],
                              op=ALU.subtract).then_inc(done, 1)

        DIAG_UNITS = ((0, 1, 2), (3, 4), (5, 6, 7), ())

        wide = [P, NT, E]

        def linked(eng, s):
            steps = [0]

            def link(ins):
                steps[0] += 1
                ins.then_inc(s, 1)
                eng.wait_ge(s, steps[0])
            return link

        def choose_experts(eng):
            link = linked(eng, s_choose)
            eng.wait_ge(s_affp, NG)
            link(eng.tensor_copy(flat(aff[:]), bank[7][:, 0:NT * E]))
            eng.tensor_reduce(amax[:], aff[:], AX.X, ALU.max).then_inc(s_amax, 1)
            eng.wait_ge(s_amax, 1)
            link(eng.tensor_tensor(hit[:], aff[:], amax[:, :].unsqueeze(2).broadcast_to(wide), ALU.is_equal))
            link(eng.tensor_tensor(hit[:], hit[:], rank_w[:, :].unsqueeze(1).broadcast_to(wide), ALU.mult))
            link(eng.tensor_reduce(posf[:], hit[:], AX.X, ALU.max))
            link(eng.tensor_tensor(onehot[:], hit[:], posf[:, :].unsqueeze(2).broadcast_to(wide), ALU.is_equal))
            eng.tensor_copy(onehot16[:], onehot[:]).then_inc(s_onehot, 1)

        def block_experts(eng):
            eng.wait_ge(s_base, 1)
            link = linked(eng, s_blocks)
            link(eng.tensor_tensor(slot_hit[:], slot[:], base[0:1, :].unsqueeze(1).broadcast_to([1, NS, E]), ALU.is_ge))
            link(eng.tensor_reduce(tile_ef[:], slot_hit[:], AX.X, ALU.add))
            eng.tensor_scalar(tile_e[:, 0:NS], tile_ef[:], -1.0, None, ALU.add).then_inc(s_tile_e, 1)

        def place_tokens(eng):
            link = linked(eng, s_sort)
            eng.wait_ge(s_cntc, 2)
            src, step = 0, 1
            while step < NT:
                link(eng.tensor_copy(cum[:, 1 - src, 0:step, :], cum[:, src, 0:step, :]))
                link(eng.tensor_tensor(cum[:, 1 - src, step:, :], cum[:, src, step:, :], cum[:, src, 0:NT - step, :], ALU.add))
                src, step = 1 - src, 2 * step
            link(eng.tensor_tensor(below[:, 1:, :], below[:, 1:, :], cum[:, src, 0:NT - 1, :], ALU.add))
            link(eng.tensor_scalar(tiles_f[:], cum[:, src, NT - 1, :], 1.0 / FW, 0.5 - 0.5 / FW, ALU.mult, ALU.add))
            link(eng.tensor_scalar(tiles_f[:], tiles_f[:], 2.0 ** 23, None, ALU.add))
            link(eng.tensor_scalar(tiles_f[:], tiles_f[:], 2.0 ** 23, None, ALU.subtract))
            link(eng.tensor_copy(tcum[:, 0, :], tiles_f[:]))
            src, step = 0, 1
            while step < E:
                link(eng.tensor_copy(tcum[:, 1 - src, 0:step], tcum[:, src, 0:step]))
                link(eng.tensor_tensor(tcum[:, 1 - src, step:], tcum[:, src, step:], tcum[:, src, 0:E - step], ALU.add))
                src, step = 1 - src, 2 * step
            link(eng.tensor_tensor(base[:], tcum[:, src, :], tiles_f[:], ALU.subtract))
            eng.sem_inc(s_base, 1)
            link(eng.tensor_scalar(base_rows[:], base[:], float(FW), None, ALU.mult))
            link(eng.tensor_tensor(below[:], below[:], base_rows[:, :].unsqueeze(1).broadcast_to(wide), ALU.add))
            link(eng.tensor_tensor(below[:], below[:], onehot[:], ALU.mult))
            n = E // 2
            while n:
                dst = below[:, :, 0:n] if n > 1 else posf[:].unsqueeze(2)
                link(eng.tensor_tensor(out=dst, in0=below[:, :, 0:n], in1=below[:, :, n:2 * n], op=ALU.add))
                n //= 2
            link(eng.tensor_copy(pos[:], posf[:]))

        block = ctx.enter_context(nc.Block())

        @block.sync
        def _(sp):
            for g in range(NG):
                sp.dma_start(x_sb[:, g * GT:(g + 1) * GT, :], x_t[:, g * GT:(g + 1) * GT, :]).then_inc(s_xin[g * NQ // NG], 16)
            for dst, src in ((b1_sb[0:E, :], b1), (b1_sb[E:2 * E, :], b1),
                             (b2_sb[0:E, :], b2), (b2_sb[E:2 * E, :], b2)):
                sp.dma_start(dst, src).then_inc(s_bias, 16)
            for e in range(E):
                wait(sp, s_w1p, e - 1)
                sp.dma_start(w1_raw[:, e % 2, :], w1[e, :, :]).then_inc(s_wl[0][e % 2], 16)
                for f in range(2 * e, min(2 * e + 2, E)):
                    wait(sp, s_w2lo, f - 1)
                    sp.dma_start(w2_raw[:, f % 2, :].rearrange("p (c d) -> p c d", d=P),
                                 w2[f, :, :].rearrange("(c p) d -> p c d", p=P)).then_inc(s_wl[1][f % 2], 16)
            sp.wait_ge(s_zero, 1)
            sp.dma_start(sorted_x.rearrange("(p a) d -> p a d", p=P),
                         zero[:, :].unsqueeze(1).broadcast_to([P, NS * FT, 2 * P])).then_inc(s_zeroed, 16)
            sp.wait_ge(s_scat, 16 * NT)
            src = sorted_x.rearrange("(k t p) d -> k p t d", p=P, t=FT)
            dst = sorted_y.rearrange("(k t p) d -> k p t d", p=P, t=FT)

            def block_of(t, k):
                return (t[bass.ds(k, 1), :, :, :]).rearrange("k p t d -> p (k t) d")

            def load_sorted(k, u):
                sp.dma_start(xs_sb[:, u, :, :], block_of(src, k)).then_inc(s_xs[u], 16)

            def store_sorted(k, u):
                sp.wait_ge(s_ysb, k + 1)
                sp.dma_start(block_of(dst, k), y_sb[:, u, :].rearrange("p (t d) -> p t d", d=P)).then_inc(s_yst[u], 16)

            def move(k, u):
                if not isinstance(k, int) or k < NS:
                    wait(sp, s_tr, k - 1)
                    load_sorted(k, u)
                if not isinstance(k, int) or k >= 4:
                    store_sorted(k - 4, u)

            for k in range(4):
                move(k, k % 2)
            with sp.Fori(2, NS // 2) as r:
                for u in range(2):
                    move(r * 2 + u, u)
            for k in range(NS - NS % 2, NS + 4):
                move(k, k % 2)
            for g in range(NG):
                if g < BG:
                    sp.wait_ge(s_sum, g + 1)
                else:
                    sp.wait_ge(s_sum_b1, g - BG + 1)
                    sp.wait_ge(s_att, 2 * (g + 1))
                sp.dma_start(out_t[:, g * GT:(g + 1) * GT, :], x_sb[:, g * GT:(g + 1) * GT, :]).then_inc(s_out, 16)
            sp.wait_ge(s_out, 16 * NG)

        @block.gpsimd
        def _(pool):
            pool.memset(zero[:], 0.0).then_inc(s_zero, 1)
            row = [[1, P]]
            pool.memset(onesf[:], 1.0).then_inc(s_core, 1)
            pool.wait_ge(s_core, 1)
            pool.affine_select(out=ident[:], in_=onesf[:], compare_op=ALU.is_equal, fill=0.0, base=0,
                               pattern=row, channel_multiplier=-1).then_inc(s_core, 1)
            pool.wait_ge(s_core, 2)
            pool.affine_select(out=CT[:], in_=ident[:], compare_op=ALU.is_gt, fill=-1.0, base=LAST,
                               pattern=[[0, P]], channel_multiplier=-1).then_inc(s_core, 1)
            pool.wait_ge(s_core, 3)
            pool.affine_select(out=CT[:], in_=CT[:], compare_op=ALU.is_gt, fill=0.0, base=LAST,
                               pattern=[[-1, P]], channel_multiplier=0).then_inc(s_core, 1)
            for dst, value in ((xa_hi[:, :, LAST:P], 1.0), (xa_lo[:, :, LAST:P], 0.0), (x2[:, :, LAST:P], 1.0),
                               (x2[:, :, 2 * P - 1:2 * P], 0.0), (neg_max[:], 0.0),
                               (pick[:], 0.0), (tile_e[:], 0)):
                pool.memset(dst, value).then_inc(s_const, 1)
            pool.iota(rank_w[:], pattern=[[-1, E]], base=E, channel_multiplier=0,
                      allow_small_or_imprecise_dtypes=True).then_inc(s_const, 1)
            pool.iota(slot[:], pattern=[[1, NS], [0, E]], base=0, channel_multiplier=0,
                      allow_small_or_imprecise_dtypes=True).then_inc(s_const, 1)
            pool.affine_select(out=ident16[:], in_=onesf[:], compare_op=ALU.is_equal, fill=0.0, base=0,
                               pattern=row, channel_multiplier=-1).then_inc(s_const, 1)
            pool.affine_select(out=upper[:], in_=onesf[:], compare_op=ALU.is_gt, fill=0.0, base=0,
                               pattern=row, channel_multiplier=-1).then_inc(s_const, 1)
            pool.affine_select(out=ones16[:], in_=onesf[:], compare_op=ALU.is_ge, fill=0.0, base=0,
                               pattern=row, channel_multiplier=0).then_inc(s_const, 1)
            pool.wait_ge(s_zero, 1)
            pool.affine_select(out=mask_qk[:], in_=zero[:, 0:P], compare_op=ALU.is_ge, fill=MASK, base=0,
                               pattern=[[-1, P]], channel_multiplier=1).then_inc(s_const, 1)
            pool.affine_select(out=mask_kq[:], in_=zero[:, 0:P], compare_op=ALU.is_ge, fill=MASK, base=0,
                               pattern=row, channel_multiplier=-1).then_inc(s_const, 1)
            n = 14
            pool.wait_ge(s_const, n)
            for k, first_row in enumerate((0, -E)):
                pool.affine_select(out=pick[:], in_=pick[:], compare_op=ALU.not_equal, fill=W_SCALE,
                                   base=first_row, pattern=[[-1, E], [0, P]], channel_multiplier=1).then_inc(s_const, 1)
                pool.wait_ge(s_const, n + 1 + k)
            pool.affine_select(out=pick_last[:], in_=pick[:], compare_op=ALU.is_ge, fill=0.0, base=-LAST,
                               pattern=[[0, E], [1, P]], channel_multiplier=0).then_inc(s_const, 1)

            def tick(t):
                if is_in(t - 1) and not by_vector(t - 1):
                    g = of(t - 1)
                    pool.wait_ge(s_xahi, g + 1)
                    pool.tensor_tensor(out=most(xa_lo, g), in0=most(xn, g), in1=most(xa_hi, g),
                                       op=ALU.subtract).then_inc(s_xalo[0], 1)
                if is_in(t):
                    pool.wait_ge(s_xa, of(t) + 1)
                    u = par(t)
                    if is_in(t - 2):
                        wait(pool, s_x2lo, of(t) - 1)
                    r2 = rs[:, 1, bass.ds(of(t) * GT, GT)].unsqueeze(2).broadcast_to([P, GT, P])
                    pool.tensor_tensor(out=x2_f[:, u, :, :],
                                       in0=xn[:, bass.ds(of(t) * GT, GT), :], in1=r2, op=ALU.mult).then_inc(s_x2f, 1)
                if is_in(t - 1):
                    g = of(t - 1)
                    pool.wait_ge(s_x2hi, g + 1)
                    to = x2[:, bass.ds(g * GT, GT), :]
                    pool.tensor_tensor(out=to[:, :, P:2 * P - 1], in0=x2_f[:, 1 - par(t), :, 0:LAST],
                                       in1=to[:, :, 0:LAST], op=ALU.subtract).then_inc(s_x2lo, 1)
                if static(t) and t.n < E // 2:
                    for e in range(2 * t.n, 2 * t.n + 2):
                        pool.wait_ge(s_w2hi, e + 1)
                        pool.tensor_tensor(out=w2_hl[:, e, F:2 * F], in0=w2_raw[:, e % 2, :], in1=w2_hl[:, e, 0:F],
                                           op=ALU.subtract).then_inc(s_w2lo, 1)

            ticks(pool, tick)

            def base(b):
                with pool.Fori(b * BG, (b + 1) * BG) as g:
                    pool.tensor_tensor(out=tile(x_g, g, GW), in0=tile(x_g, g, GW), in1=tile(xn_g, g, GW),
                                       op=ALU.add).then_inc(s_basep, 1)

            base(0)
            for n in range(LOW_POOL):
                weights_low(pool, n, n % 2, n * P if n < GT else 0)
            place_tokens(pool)
            pool.wait_ge(s_x2lo, NG)
            pool.wait_ge(s_zeroed, 16)
            for i in range(NT):
                pool.indirect_dma_start(out=sorted_x[:, :], out_offset=bass.IndirectOffsetOnAxis(
                    ap=pos[:, i:i + 1], axis=0), in_=x2[:, i, :], in_offset=None).then_inc(s_scat, 16)
            base(1)
            pool.wait_ge(s_basep, NG)
            for u in range(2):
                pool.wait_ge(s_yst[u], 16 * ((NS + 1 - u) // 2))
            for i in range(NT):
                pool.indirect_dma_start(out=yg[:, i, :], out_offset=None, in_=sorted_y[:, :],
                                        in_offset=bass.IndirectOffsetOnAxis(
                                            ap=pos[:, i:i + 1], axis=0)).then_inc(s_gath[i // BT], 16)
            pool.wait_ge(s_gath[0], 16 * BT)
            yg_g = yg[:].rearrange("p (g t) d -> p g (t d)", t=GT)
            with pool.Fori(0, BG) as g:
                y = yg[:, bass.ds(g * GT, GT), :]
                pool.tensor_tensor(out=y, in0=y, in1=alpha[:, bass.ds(g * GT, GT)].unsqueeze(2).broadcast_to([P, GT, P]),
                                   op=ALU.mult).then_inc(s_yal, 1)
                pool.wait_ge(s_yal, g + 1)
                pool.wait_ge(s_att, g * 2 + 2)
                pool.tensor_tensor(out=tile(x_g, g, GW), in0=tile(x_g, g, GW), in1=tile(yg_g, g, GW),
                                   op=ALU.add).then_inc(s_sum, 1)

        N_CONST = 17
        N_SMALL = 5
        H = NT // NQ

        @block.vector
        def _(v):
            chain = [0]

            def link(ins):
                chain[0] += 1
                ins.then_inc(s_dve, 1)
                v.wait_ge(s_dve, chain[0])

            def statistics(h):
                v.wait_ge(s_xin[h], 16 * NG // NQ)
                for t in range(h * H, (h + 1) * H):
                    v.bn_stats(stats[:, t, :], x_sb[:, t, :]).then_inc(s_bn, 1)
                v.wait_ge(s_bn, (h + 1) * H)
                for t in range(h * H, (h + 1) * H):
                    v.bn_aggr(mv[:, t, :], stats[:, t, :]).then_inc(s_ag, 1)
                v.wait_ge(s_ag, (h + 1) * H)

            def variances(h):
                a = slice(h * H, (h + 1) * H)
                var = mv[:, a, 1:2].rearrange("p a b -> p (a b)")
                link(v.tensor_scalar(vs[:, 0, 0, a], var, EPS, None, ALU.add))
                link(v.reciprocal(nw[:, 0, 0, a], vs[:, 0, 0, a]))
                link(v.tensor_tensor(nw[:, 0, 1, a], nw[:, 0, 0, a], var, ALU.mult))
                v.tensor_scalar(vs[:, 0, 1, a], nw[:, 0, 1, a], EPS, None, ALU.add).then_inc(s_dve_roots, 1)

            def inverse_roots(h):
                a = slice(h * H, (h + 1) * H)
                v.wait_ge(s_actc, h + 1)
                v.wait_ge(s_dve_roots, h + 1)
                link(v.reciprocal(rs[:, :, a], vs[:, 1, :, a]))
                link(v.tensor_tensor(nw[:, 0, :, a], rs[:, :, a], rs[:, :, a], ALU.mult))
                link(v.tensor_tensor(nw[:, 1, :, a], nw[:, 0, :, a], vs[:, 0, :, a], ALU.mult))
                link(v.tensor_scalar(nw[:, 0, :, a], nw[:, 1, :, a], -0.5, 1.5, ALU.mult, ALU.add))
                link(v.tensor_tensor(rs[:, :, a], rs[:, :, a], nw[:, 0, :, a], ALU.mult))

            statistics(0)
            variances(0)
            v.wait_ge(s_core, 4)
            v.wait_ge(s_small, 1)
            v.tensor_copy(smallT[:], bank[0][:, 0:24]).then_inc(s_smallc, 1)
            v.tensor_copy(U_sb[:], bank[1][:, 0:P]).then_inc(s_smallc, 1)
            v.tensor_copy(ovC[:, 0:P], bank[2][:, 0:P]).then_inc(s_smallc, 1)
            v.tensor_copy(ovC[:, P:P + 1], ident[:, LAST:P]).then_inc(s_smallc, 1)
            inverse_roots(0)
            v.wait_ge(s_const, N_CONST)

            def folded():
                v.wait_ge(s_small, 2)
                v.tensor_scalar(G_hi[:], bank[3][:, 0:P], QK_SCALE, None, ALU.mult).then_inc(s_halves, 1)
                v.tensor_scalar(cent_hi[:], bank[4][:, 0:E], QK_SCALE, None, ALU.mult).then_inc(s_halves, 1)
                v.wait_ge(s_halves, 2)
                v.scalar_tensor_tensor(out=G_lo[:], in0=bank[3][:, 0:P], scalar=QK_SCALE, in1=G_hi[:],
                                       op0=ALU.mult, op1=ALU.subtract).then_inc(s_smallc, 1)
                v.scalar_tensor_tensor(out=cent_lo[:], in0=bank[4][:, 0:E], scalar=QK_SCALE, in1=cent_hi[:],
                                       op0=ALU.mult, op1=ALU.subtract).then_inc(s_smallc, 1)

            def bias_halves():
                v.wait_ge(s_bias_hi, 2)
                for raw, hi, hl in ((b1_sb, b1_hi, b1_hl), (b2_sb, b2_hi, b2_hl)):
                    link(v.scalar_tensor_tensor(out=hl[:], in0=raw[:], scalar=W_SCALE, in1=hi[:],
                                                op0=ALU.mult, op1=ALU.subtract))
                    v.tensor_copy(hl[0:E, :], hi[0:E, :]).then_inc(s_bias_hl, 1)

            def reduce_unit(n, where, i, c, width):
                v.wait_ge(s_max_mm, n + 1)
                v.tensor_reduce(row_max[:, i, c:c + 1] if isinstance(c, int) else row_max[:, i, bass.ds(c, 1)],
                                bank[where][:, 0:width], AX.X, ALU.max).then_inc(s_max, 1)

            def row_maxima(b, g, units_done):
                v.wait_ge(s_max, units_done)
                if g:
                    link(v.tensor_reduce(row_m[:], row_max[:, :, 0:g + 1], AX.X, ALU.max))
                    m = row_m[:]
                else:
                    m = row_max[:, :, 0]
                v.tensor_scalar(neg_max[:, :, LAST], m, -1.0, SHIFT, ALU.mult, ALU.add).then_inc(s_neg, 1)

            def shift(b, g, where=5):
                v.wait_ge(s_negT, b * BG + g + 1)
                q = qT_hi[96:P, (b * BG + g) * GW:(b * BG + g + 1) * GW]
                v.tensor_tensor(q, q, bank[where][96:P, :], ALU.add).then_inc(s_shift, 1)

            def tick(t):
                if is_in(t):
                    g, grp = of(t), [P, GT, P]
                    on = bass.ds(g * GT, GT)
                    to = xn[:, on, :]
                    if isinstance(g, int):
                        for i in range(g * GT, (g + 1) * GT):
                            ins = v.tensor_scalar(xn[:, i, :], x_sb[:, i, :], mv[:, i, 0:1], rs[:, 0, i:i + 1],
                                                  ALU.subtract, ALU.mult)
                        ins.then_inc(s_xa, 1)
                    else:
                        v.tensor_tensor(to, x_sb[:, on, :], mv[:, on, 0:1].broadcast_to(grp), ALU.subtract).then_inc(s_centred, 1)
                        v.wait_ge(s_centred, g - (LAGS - 1))
                        v.tensor_tensor(to, to, rs[:, 0, on].unsqueeze(2).broadcast_to(grp), ALU.mult).then_inc(s_xa, 1)
                if is_in(t - 1) and by_vector(t - 1):
                    g = of(t - 1)
                    v.wait_ge(s_xahi, g + 1)
                    v.tensor_tensor(most(xa_lo, g), most(xn, g), most(xa_hi, g), ALU.subtract).then_inc(s_xalo[1], 1)
                if is_in(t - 2):
                    g = of(t - 2)
                    v.wait_ge(s_w1hi, g + 1)
                    v.scalar_tensor_tensor(out=tile(w1_hl, g)[:, F:2 * F], in0=bank[5 + par(t)][:], scalar=1.0 / W_SCALE,
                                           in1=tile(w1_hl, g)[:, 0:F], op0=ALU.mult, op1=ALU.subtract).then_inc(s_w1lo, 1)
                if is_in(t):
                    g = of(t)
                    A = A_e[:, par(t), :]
                    v.tensor_scalar(A, CT[:], smallT[:, bass.ds(g + E, 1)], W_SCALE * W_SCALE, ALU.mult,
                                    ALU.mult).then_inc(s_Aw, 1)
                    v.wait_ge(s_Aw, g + 1)
                    v.tensor_scalar(A[:, LAST:P], smallT[:, bass.ds(g + 2 * E, 1)], W_SCALE * W_SCALE, None,
                                    ALU.mult).then_inc(s_Ae, 1)
                if is_in(t - 4):
                    g = of(t - 4)
                    v.wait_ge(s_qhi, g + 1)
                    v.scalar_tensor_tensor(out=cols(qT_lo, g), in0=bank[2 + par(t)][:], scalar=1.0 / QK_SCALE,
                                           in1=cols(qT_hi, g), op0=ALU.mult, op1=ALU.subtract).then_inc(s_qlo, 1)
                for i in first_units(t):
                    reduce_unit(i, 4, i, 0, (i + 1) * P)
                if static(t) and t.n == NG + LAGS - 1:
                    row_maxima(0, 0, GT)
                    shift(0, 0, 4)
                if static(t) and t.n == 0:
                    folded()
                    bias_halves()
                if static(t) and t.n < NQ:
                    if t.n:
                        inverse_roots(t.n)
                    if t.n + 1 < NQ:
                        statistics(t.n + 1)
                        variances(t.n + 1)

            ticks(v, tick)
            choose_experts(v)
            def quotients(b, g, halves=(0, 1)):
                for f in halves:
                    n = (b * BG + g) * 2 + f
                    v.wait_ge(s_basep, b * BG + g + 1)
                    v.wait_ge(s_fin, n + 1)
                    o = bank[6 + f][:, 0:2 * (P + 1)].rearrange("p (t d) -> p t d", t=2)
                    wait(v, s_att, n - 1)
                    link(v.reciprocal(inv_den[:, f, :], o[:, :, P]))
                    for t in range(2):
                        dst = x_sb[:, (b * BG + g) * GT + f * 2 + t, :]
                        ins = v.scalar_tensor_tensor(out=dst, in0=o[:, t, 0:P], scalar=inv_den[:, f, t:t + 1], in1=dst,
                                                     op0=ALU.mult, op1=ALU.add)
                    ins.then_inc(s_att, 1)

            def turned(k, u):
                v.wait_ge(s_tr, k + 1)
                v.tensor_copy(x2T[:, u, :], bank[6][:].bitcast(F16)[:, 0:2 * FW]).then_inc(s_x2T, 1)

            def sigmoids():
                v.wait_ge(s_actc, NQ + 1)
                link(v.tensor_scalar(eneg[:], eneg[:], 1.0, None, ALU.add))
                link(v.reciprocal(alpha[:], eneg[:]))

            def weigh_rows(g):
                v.wait_ge(s_gath[1], 16 * BT)
                v.wait_ge(s_basep, NG)
                v.wait_ge(s_att, 2 * (NG - 1))
                for i in range(g * GT, (g + 1) * GT):
                    ins = v.scalar_tensor_tensor(out=x_sb[:, i, :], in0=yg[:, i, :], scalar=alpha[:, i:i + 1],
                                                 in1=x_sb[:, i, :], op0=ALU.mult, op1=ALU.add)
                ins.then_inc(s_sum_b1, 1)

            def attention(b):
                n0 = b * STEPS
                u0 = n0 + GT
                for g in range(BG):
                    more = g + 1 < BG and b == 0

                    def unit(k):
                        i, c = k % GT, g + k // GT
                        reduce_unit(u0 + g * GT + k, 2 + i % 2, i, c, GW if c == g else (i + 1) * P)

                    def chunk(c, first=False):
                        for i in range(GT):
                            if more:
                                reduce_unit(c * GT + (u0 + i), 2 + i % 2, i, c, GW)
                            if not (first and n0 + i < LOW_POOL):
                                weights_low(v, c * GT + (n0 + i), i % 2, 0)
                            if first and i - b in (0, 1):
                                quotients(b, g - 1, (i - b,))
                            if first and b == 0 and g == BG - 1 and i == 2:
                                block_experts(v)
                            if first and b == 0 and g == BG - 1 and i == 3:
                                sigmoids()

                    if g:
                        chunk(0, first=True)
                    if g > 1:
                        with v.Fori(1, g) as c:
                            chunk(c)
                    for i in range(GT):
                        units = DIAG_UNITS[i] if more else ()
                        for k in units[:1]:
                            unit(k)
                        if more and i == GT - 1:
                            u0 += GT * (g + 2)
                            row_maxima(b, g + 1, u0)
                        if n0 + g * GT + i >= LOW_POOL:
                            weights_low(v, n0 + g * GT + i, i % 2, i * P)
                        if b == 1 and g == BG - 1:
                            weigh_rows(BG + i)
                        if b == 0 and g == BG - 1 and i >= GT - 2:
                            turned(i - (GT - 2), i % 2)
                        for k in units[1:]:
                            unit(k)
                    if more:
                        shift(b, g + 1)
                    n0 += GT * (g + 1)
                if b == 1:
                    v.wait_ge(s_sum_b1, BG)
                quotients(b, BG - 1)

            def ffn():
                def lows(k, u):
                    v.wait_ge(s_hhi, k + 1)
                    v.scalar_tensor_tensor(out=h_lo[:, u, :], in0=hidden_ps[u], scalar=0.0, in1=h_hi[:, u, :],
                                           op0=ALU.max, op1=ALU.subtract).then_inc(s_hlo, 1)

                def unit(n, g, c, i, width):
                    reduce_unit(n, 7, i, c, width or GW)
                    if c == g and i == GT - 1:
                        row_maxima(1, g, n + 1)

                lows(0, 0)
                turned(2, 0)
                lows(1, 1)
                for m in range(NS - 1):
                    for work in max_work(m, unit, lambda g: shift(1, g, 7)):
                        work()
                    if m + 3 < NS:
                        turned(m + 3, (m + 1) % 2)
                    if m + 2 < NS:
                        lows(m + 2, m % 2)

            attention(0)
            ffn()
            attention(1)

        @block.scalar
        def _(a):
            for dst, src in ((small[0:8, :], cent), (small[8:16, :], ln_g), (small[16:24, :], ln_b),
                             (qk_sb[:], qk), (ov_sb[:], ov)):
                a.dma_start(dst, src).then_inc(s_win, 16)

            def roots(h):
                t = slice(h * H, (h + 1) * H)
                a.wait_ge(s_dve_roots, h + 1)
                a.activation(vs[:, 1, :, t], vs[:, 0, :, t], ACT.Sqrt).then_inc(s_actc, 1)

            roots(0)
            a.wait_ge(s_bias, 16 * 4)
            a.activation(b1_hi[:], b1_sb[:], ACT.Copy, scale=W_SCALE).then_inc(s_bias_hi, 1)
            a.activation(b2_hi[:], b2_sb[:], ACT.Copy, scale=W_SCALE).then_inc(s_bias_hi, 1)

            def tick(t):
                if is_in(t):
                    g = of(t)
                    a.wait_ge(s_xa, g + 1)
                    a.activation(most(xa_hi, g), most(xn, g), ACT.Copy).then_inc(s_xahi, 1)
                if is_in(t - 2):
                    g = of(t - 2)
                    a.wait_ge(s_kp, g + 1)
                    for half, to, s in ((0, kT_hi, s_khi), (1, kT_lo, s_klo)):
                        a.activation(cols(to, g), bank[par(t)][:].bitcast(F16)[:, half * GW:(half + 1) * GW],
                                     ACT.Copy).then_inc(s, 1)
                if is_in(t - 1):
                    g = of(t - 1)
                    a.wait_ge(s_w1p, g + 1)
                    a.activation(tile(w1_hl, g)[:, 0:F], bank[5 + par(t - 1)][:], ACT.Copy, scale=1.0 / W_SCALE).then_inc(s_w1hi, 1)
                    a.wait_ge(s_x2f, g + 1)
                    a.activation(x2[:, bass.ds(g * GT, GT), 0:LAST], x2_f[:, par(t - 1), :, 0:LAST], ACT.Copy).then_inc(s_x2hi, 1)
                if is_in(t - 3):
                    g = of(t - 3)
                    a.wait_ge(s_qp, g + 1)
                    a.activation(cols(qT_hi, g), bank[2 + par(t - 3)][:], ACT.Copy, scale=1.0 / QK_SCALE).then_inc(s_qhi, 1)
                if static(t) and t.n < E // 2:
                    for e in range(2 * t.n, 2 * t.n + 2):
                        u = e % 2
                        a.wait_ge(s_wl[1][u], (e - u) * 8 + 16)
                        a.activation(w2_raw[:, u, :], w2_raw[:, u, :], ACT.Copy, scale=W_SCALE).then_inc(s_w2s, 1)
                        a.wait_ge(s_w2s, e + 1)
                        a.activation(w2_hl[:, e, 0:F], w2_raw[:, u, :], ACT.Copy).then_inc(s_w2hi, 1)
                if static(t) and t.n + 1 < NQ:
                    roots(t.n + 1)

            ticks(a, tick)

            def counts():
                a.wait_ge(s_cnt, 1)
                a.activation(flat(cum[:, 0, :, :]), bank[5][:, NT * E:2 * NT * E], ACT.Copy).then_inc(s_cntc, 1)
                a.activation(flat(below[:]), bank[5][:, 0:NT * E], ACT.Copy).then_inc(s_cntc, 1)

            def exp_step(n, par, off):
                a.wait_ge(s_sc, n + 1)
                wait(a, s_pv, n - 1)
                if not isinstance(n, int) or n >= 2:
                    a.wait_ge(*lows_done(n - 2))
                a.activation(p_hi[:, par, off:GW], bank[par][:, off:GW], ACT.Exp, scale=SCALE).then_inc(s_phi, 1)
                a.activation(p_sb[:, par, off:GW], bank[par][:, off:GW], ACT.Exp, scale=SCALE).then_inc(s_exp, 1)

            def sums_out(b, g, steps):
                a.wait_ge(s_pvlo, steps)
                if b * BG + g:
                    a.wait_ge(s_fin, 2 * (b * BG + g))
                a.activation(oT[:], sum_bank(b, g)[:], ACT.Copy).then_inc(s_oT, 1)

            def attention(b):
                n0 = b * STEPS
                for g in range(BG):
                    if b == 1 and g:
                        exp_step(n0, 0, 0)
                        sums_out(b, g - 1, n0)
                    if g:
                        for i in range(b, GT):
                            exp_step(n0 + i, i % 2, 0)
                    if g > 1:
                        with a.Fori(1, g) as c:
                            for i in range(GT):
                                exp_step(c * GT + (n0 + i), i % 2, 0)
                    if b == 0 and g == 1:
                        counts()
                    if b == 0 and g == BG - 2:
                        a.activation(eneg[:], amax[:], ACT.Exp, scale=-1.0 / QK_SCALE).then_inc(s_actc, 1)
                    for i in range(GT):
                        exp_step(n0 + g * GT + i, i % 2, i * P)
                    n0 += GT * (g + 1)
                    if b == 0 or g == BG - 1:
                        sums_out(b, g, n0)

            def ffn():
                def highs(k, u):
                    a.wait_ge(s_z, k + 1)
                    a.activation(h_hi[:, u, :], hidden_ps[u], ACT.Relu).then_inc(s_hhi, 1)

                def rows(k, u):
                    a.wait_ge(s_y, k + 1)
                    if not isinstance(k, int) or k >= 2:
                        a.wait_ge(s_yst[u], (k - u) * 8)
                    a.activation(y_sb[:, u, :], bank[4 + u][:, 0:FT * P], ACT.Copy,
                                 scale=1.0 / (W_SCALE * W_SCALE)).then_inc(s_ysb, 1)

                def both(k, u):
                    if not isinstance(k, int) or k + 1 < NS:
                        highs(k + 1, 1 - u)
                    rows(k, u)

                highs(0, 0)
                for k in range(2):
                    both(k, k)
                with a.Fori(1, NS // 2) as r:
                    for u in range(2):
                        both(r * 2 + u, u)
                for k in range(NS - NS % 2, NS):
                    both(k, k % 2)

            attention(0)
            ffn()
            attention(1)

        @block.tensor
        def _(pe):
            pe.wait_ge(s_core, 4)
            pe.wait_ge(s_win, 16 * N_SMALL)
            mm = pe.matmul
            pe.transpose(bank[0][:, 0:24], small[:], ident[0:24, 0:24])
            mm(bank[1][:, 0:P], qk_sb[:], CT[:], start=True, stop=True)
            mm(bank[2][:, 0:P], CT[:], ov_sb[:], start=True, stop=True).then_inc(s_small, 1)
            pe.wait_ge(s_smallc, 4)
            mm(bank[4][:, 0:E], CT[:], smallT[:, 0:E], start=True, stop=True)
            mm(bank[3][:, 0:P], U_sb[:], CT[:], start=True, stop=True).then_inc(s_small, 1)
            pe.wait_ge(s_smallc, 6)
            pe.wait_ge(s_const, N_CONST)

            def max_unit(n, b, g, where, i, c, width, ring=2):
                wait(pe, s_max, n + 1 - ring)
                q = (b * BG + g) * GW + i * P
                diag = width is not None
                w = width or GW
                m = mm(bank[where][:, 0:w], qT_hi[:, q:q + P], kT_hi[:, bass.ds(c * GW + b * S, w)], start=True,
                       stop=not diag)
                if diag:
                    m = mm(bank[where][:, w - P:w], ident16[:], mask_qk[:], start=False, stop=True)
                m.then_inc(s_max_mm, 1)

            def shift(b, g, where=5):
                nth = b * BG + g
                if nth == 2:
                    pe.wait_ge(s_cntc, 2)
                pe.wait_ge(s_neg, nth + 1)
                for i in range(GT):
                    t = mm(bank[where][:, i * P:(i + 1) * P], neg_max[:, i, :], ident16[:], start=True, stop=True)
                t.then_inc(s_negT, 1)

            def tick(t):
                if is_in(t - 3):
                    g = of(t - 3)
                    pe.wait_ge(s_klo, g + 1)
                    if is_in(t - 5):
                        pe.wait_ge(s_qlo, g - 1)
                    q = bank[2 + par(t - 3)][:]
                    mm(q, G_hi[:], cols(kT_hi, g), start=True, stop=False)
                    mm(q, G_hi[:], cols(kT_lo, g), start=False, stop=False)
                    mm(q, G_lo[:], cols(kT_hi, g), start=False, stop=True).then_inc(s_qp, 1)
                    for i in range(GT):
                        hi, lo = (k[:, bass.ds(g * GW + i * P, P)] for k in (kT_hi, kT_lo))
                        to = bank[7][:, bass.ds(g * (GT * E) + i * E, E)]
                        mm(to, hi, cent_hi[:], start=True, stop=False)
                        mm(to, hi, cent_lo[:], start=False, stop=False)
                        m = mm(to, lo, cent_hi[:], start=False, stop=True)
                    m.then_inc(s_affp, 1)
                if is_in(t - 2):
                    g = of(t - 2)
                    if by_vector(t - 2):
                        pe.wait_ge(s_xalo[1], 1)
                    else:
                        pe.wait_ge(s_xalo[0], g + 1)
                    for half, x16 in enumerate((xa_hi, xa_lo)):
                        for i in range(GT):
                            c = half * GW + i * P
                            m = pe.transpose(bank[par(t)][:].bitcast(F16)[:, c:c + P], tile(x16, g * GT + i), ident16[:])
                    m.then_inc(s_kp, 1)
                if is_in(t):
                    g, u = of(t), par(t)
                    pe.wait_ge(s_Ae, g + 1)
                    pe.wait_ge(s_bias_hl, 2)
                    pe.wait_ge(s_wl[0][u], (g - u) * 8 + 16)
                    if is_in(t - 2):
                        pe.wait_ge(s_w1lo, g - 1)
                    mm(bank[5 + u][:], A_e[:, u, :], w1_raw[:, u, :], start=True, stop=False)
                    mm(bank[5 + u][:], tile(pick_last, g), b1_hl[:], start=False, stop=True).then_inc(s_w1p, 1)
                for i in first_units(t):
                    max_unit(i, 0, 0, 4, i, 0, (i + 1) * P, ring=1)
                if static(t) and t.n == NG + LAGS - 1:
                    shift(0, 0, 4)

            ticks(pe, tick)
            pe.wait_ge(s_w1lo, E)
            pe.wait_ge(s_qlo, NG)

            def counts():
                pe.wait_ge(s_onehot, 1)
                oh = flat(onehot16[:])
                mm(bank[5][:, 0:NT * E], upper[:], oh, start=True, stop=True)
                mm(bank[5][:, NT * E:2 * NT * E], ones16[:], oh, start=True, stop=True).then_inc(s_cnt, 1)

            def scores(n, b, g, par, j, off):
                wait(pe, s_exp, n - 1)
                q = slice((b * BG + g) * GW + off, (b * BG + g + 1) * GW)
                k = bass.ds(j * P + b * S, P) if not isinstance(j, int) else slice(b * S + j * P, b * S + (j + 1) * P)
                dst = bank[par][:, off:GW]
                mm(dst, kT_hi[:, k], qT_hi[:, q], start=True, stop=False)
                mm(dst, kT_hi[:, k], qT_lo[:, q], start=False, stop=False)
                diag = isinstance(j, int) and j >= g * GT
                m = mm(dst, kT_lo[:, k], qT_hi[:, q], start=False, stop=not diag)
                if diag:
                    m = mm(bank[par][:, off:off + P], ident16[:], mask_kq[:], start=False, stop=True)
                m.then_inc(s_sc, 1)

            def rows(t, b, j):
                return tile(t, j + b * BT)

            def weighted(n, b, g, par, j, off):
                first = isinstance(j, int) and j == 0
                if first:
                    wait(pe, s_oT, b * BG + g - (b and g > 0))
                pe.wait_ge(s_phi, n + 1)
                to, w = sum_bank(b, g)[:, off:GW], p_hi[:, par, off:GW]
                mm(to, rows(xa_hi, b, j), w, start=first, stop=False, skip_group_check=True)
                mm(to, rows(xa_lo, b, j), w, start=False, stop=False, skip_group_check=True).then_inc(s_pv, 1)

            def weighted_low(n, b, g, par, j, off):
                pe.wait_ge(*lows_done(n))
                last = isinstance(j, int) and j == g * GT + GT - 1
                mm(sum_bank(b, g)[:, off:GW], rows(xa_hi, b, j), p_lo[:, par, off:GW], start=False, stop=last,
                   skip_group_check=True).then_inc(s_pvlo, 1)

            def project(b, g):
                nth = b * BG + g
                if nth == 0:
                    pe.wait_ge(s_choose, 1)
                pe.wait_ge(s_oT, nth + 1)
                if nth:
                    pe.wait_ge(s_att, 2 * nth)
                for f in range(2):
                    for t in range(2):
                        i = f * 2 + t
                        m = mm(bank[6 + f][:, t * (P + 1):(t + 1) * (P + 1)], oT[:, i * P:(i + 1) * P], ovC[:],
                               start=True, stop=True)
                    m.then_inc(s_fin, 1)

            def turn(k, u):
                wait(pe, s_x2T, k)
                pe.wait_ge(s_xs[u], (k - u) * 8 + 16)
                for half in range(2):
                    for t in range(FT):
                        m = pe.transpose(bank[6][:].bitcast(F16)[:, half * FW + t * P:half * FW + (t + 1) * P],
                                         xs_sb[:, u, t, half * P:(half + 1) * P], ident16[:])
                m.then_inc(s_tr, 1)

            def attention(b):
                n0 = b * STEPS
                u0 = n0 + GT
                for g in range(BG):
                    more = g + 1 < BG and b == 0

                    def unit(k):
                        i, c = k % GT, g + k // GT
                        max_unit(u0 + g * GT + k, b, g + 1, 2 + i % 2, i, c, None if c == g else (i + 1) * P)

                    def step(c, i, first=False):
                        j = c * GT + i
                        on = isinstance(c, int) and c == g
                        units = DIAG_UNITS[i] if more and on else ()
                        if not (on and i == GT - 1):
                            scores(j + (n0 + 1), b, g, (i + 1) % 2, j + 1, (i + 1) * P if on else 0)
                        elif b == 1 and g + 1 < BG:
                            scores(n0 + GT * (g + 1), b, g + 1, 0, 0, 0)
                        if b == 0 and g == BG - 1 and on and i >= GT - 2:
                            pe.wait_ge(s_att, 2 * g)
                            turn(i - (GT - 2), i % 2)
                        if more and not on:
                            max_unit(j + u0, b, g + 1, 2 + i % 2, i, c, None)
                        for k in units[:1]:
                            unit(k)
                        if g and isinstance(c, int) and (c, i) == (0, b):
                            project(b, g - 1)
                        if not first:
                            weighted_low(j + (n0 - 1), b, g, (i + 1) % 2, j - 1, (i - 1) * P if on and i else 0)
                        for k in units[1:2]:
                            unit(k)
                        weighted(j + n0, b, g, i % 2, j, i * P if on else 0)
                        for k in units[2:]:
                            unit(k)

                    if b == 0:
                        pe.wait_ge(s_shift, g + 1)
                        scores(n0, b, g, 0, 0, 0)
                    for i in range(GT - 1 if g else GT):
                        step(0, i, first=(i == 0))
                    if g > 1:
                        with pe.Fori(1, g) as c:
                            step(c - 1, GT - 1)
                            for i in range(GT - 1):
                                step(c, i)
                    if b == 0 and g == 1:
                        counts()
                    if g:
                        step(g - 1, GT - 1)
                        for i in range(GT):
                            step(g, i)
                    if more:
                        shift(b, g + 1)
                    u0 += GT * (g + 2)
                    n0 += GT * (g + 1)
                    weighted_low(n0 - 1, b, g, 1, g * GT + GT - 1, (GT - 1) * P)
                if b == 1:
                    project(b, BG - 1)

            def ffn():

                def hidden(k, u, e):
                    pe.wait_ge(s_x2T, k + 1)
                    wait(pe, s_hlo, k - 1)
                    for c in range(FC):
                        dst = hidden_ps[u][:, c * FW:(c + 1) * FW]
                        hi = w1_flat[:, bass.ds(e * (2 * F) + c * P, P)]
                        lo = w1_flat[:, bass.ds(e * (2 * F) + (F + c * P), P)]
                        mm(dst, hi, x2T[:, u, 0:FW], start=True, stop=False)
                        mm(dst, hi, x2T[:, u, FW:2 * FW], start=False, stop=False)
                        m = mm(dst, lo, x2T[:, u, 0:FW], start=False, stop=True)
                    m.then_inc(s_z, 1)

                HEAD = 4

                def output(k, u, e):
                    wait(pe, s_ysb, k - 1)
                    pe.wait_ge(s_hlo, k + 1)
                    to = [bank[4 + u][:, t * P:(t + 1) * P] for t in range(FT)]
                    biases = pick[:].rearrange("k e d -> k (e d)")[:, bass.ds(e * P, P)]
                    for t in range(FT):
                        mm(to[t], biases, b2_hl[:], start=(t == 0), stop=False, skip_group_check=True)
                    for c in range(FC):
                        hi = w2_flat[:, bass.ds(e * (2 * F) + c * P, P)]
                        lo = w2_flat[:, bass.ds(e * (2 * F) + (F + c * P), P)]
                        for t in range(FT):
                            at = slice(c * FW + t * P, c * FW + (t + 1) * P)
                            mm(to[t], h_hi[:, u, at], hi, start=False, stop=False, skip_group_check=True)
                            mm(to[t], h_hi[:, u, at], lo, start=False, stop=False, skip_group_check=True)
                            m = mm(to[t], h_lo[:, u, at], hi, start=False, stop=(c == FC - 1), skip_group_check=True)
                    m.then_inc(s_y, 1)

                def experts(first, n):
                    _, values = nc.values_load_multi_w_load_instructions(
                        tile_e[0:1, first:first + n], engines=[mybir.EngineType.PE], min_val=0, max_val=E - 1,
                        skip_runtime_bounds_check_because="a count of at most E experts, less one")
                    return values

                def output_hidden(m, after_output, after_hidden):
                    u = m % 2
                    output(m, u, e[m])
                    after_output()
                    hidden(m + 2, u, e[m + 2])
                    after_hidden()
                    if m + 3 < NS:
                        turn(m + 3, 1 - u)

                pe.wait_ge(s_tile_e, 1)
                e = experts(0, HEAD)
                pe.wait_ge(s_max, STEPS)
                hidden(0, 0, e[0])
                pe.wait_ge(s_x2T, 2)
                project(0, BG - 1)
                pe.wait_ge(s_exp, STEPS)
                hidden(1, 1, e[1])
                e += experts(HEAD, NS - HEAD)
                pe.wait_ge(s_att, 2 * BG)
                turn(2, 0)
                def unit(n, g, c, i, width):
                    if c == 0 and i == 0 and g:
                        pe.wait_ge(s_shift, BG + g)
                    max_unit(n, 1, g, 7, i, c, width, ring=1)

                for m in range(NS - 2):
                    output_hidden(m, *max_work(m, unit, lambda g: shift(1, g, 7)))
                last_unit, last_shift = max_work(NS - 2, unit, lambda g: shift(1, g, 7))
                output(NS - 2, NS % 2, e[NS - 2])
                last_unit()
                pe.wait_ge(s_hlo, NS - 1)
                pe.wait_ge(s_shift, BG + 1)
                scores(STEPS, 1, 0, 0, 0, 0)
                last_shift()
                output(NS - 1, 1 - NS % 2, e[NS - 1])
                pe.wait_ge(s_shift, 2 * BG)
                pe.wait_ge(s_ysb, NS - 1)

            attention(0)
            ffn()
            attention(1)


_INS = ['L0_attn_input_data', 'L0_attn_qk', 'L0_attn_ov', 'L0_ffn_centroids', 'L0_ffn_ln_g', 'L0_ffn_ln_b',
        'L0_ffn_w1', 'L0_ffn_b1', 'L0_ffn_w2', 'L0_ffn_b2']


def kernel(**inputs):
    import numpy as _np
    import concourse.bacc as _bacc
    from concourse import mybir as _mybir
    from concourse.bass_utils import run_bass_kernel_spmd as _run

    nc = _bacc.Bacc("TRN2", target_bir_lowering=False, num_devices=1)
    arrays, args = {}, []
    for name in _INS:
        a = _np.ascontiguousarray(inputs[name])
        arrays[f"in_{name}"] = a
        args.append(nc.dram_tensor(f"in_{name}", a.shape, _mybir.dt.from_np(a.dtype), kind="ExternalInput").ap())
    B, S, D = inputs['L0_attn_input_data'].shape
    E = inputs['L0_ffn_w1'].shape[0]
    rows = B * S + (E - 1) * 256
    args.append(nc.dram_tensor("sorted_x", (rows, 2 * D), _mybir.dt.float16, kind="Internal").ap())
    args.append(nc.dram_tensor("sorted_y", (rows, D), _mybir.dt.float32, kind="Internal").ap())
    args.append(nc.dram_tensor("out", (B, S, D), _mybir.dt.float32, kind="ExternalOutput").ap())
    build(nc, *args)
    r = _run(nc, [arrays], core_ids=[0])
    return r.results[0]["out"]
```
